# Optimizing a Trainium2 kernel written in Bass

```python
import numpy as np
import jax
import jax.numpy as jnp

def _softmax(x, axis=-1):
    return jax.nn.softmax(x, axis=axis)

def _gelu(x):
    return jax.nn.gelu(x, approximate=True)

def _silu(x):
    return jax.nn.silu(x)

def _sigmoid(x):
    return jax.nn.sigmoid(x)

def _layernorm(x, axis=-1, eps=1e-05):
    m = jnp.mean(x, axis=axis, keepdims=True)
    v = jnp.var(x, axis=axis, keepdims=True)
    return (x - m) / jnp.sqrt(v + eps)

def _scatter_add(tgt, idx, src, axis=0):
    return tgt.at[idx].add(src)

def _segment_sum(src, seg, n):
    return jax.ops.segment_sum(src, seg, n)
kernel_name = 'mk_adj_ffn_d2_adj_r2_b73b27'

def setup_inputs(seed: int=0):
    np.random.seed(seed)
    _w = jnp.asarray

    def _rec_inputs():
        import jax
        import jax.numpy as jnp
        _gk = jax.random.key(seed)
        x = -0.001547 + 1.001 * jax.random.normal(jax.random.fold_in(_gk, 1), (512, 128), jnp.float32)
        _w = (1.0 + jnp.arange(512, dtype=jnp.float32)) ** (-0.5)
        _w = _w / _w.mean()
        _pij = jnp.clip(0.03125 * _w[:, None] * _w[None, :], 0.0, 1.0)
        _a = jax.random.uniform(jax.random.fold_in(_gk, 2), (512, 512)) < _pij
        adj = _a.astype(jnp.int32)
        return (x, adj)
    x, adj = _rec_inputs()

    def _L0_gnn_setup():
        import jax, jax.numpy as jnp
        import numpy as np
        BT, BN, D, H = (512, 512, 128, 8)
        DH = D // H
        key = jax.random.key(seed)
        ks = jax.random.split(key, 16)
        s = 1.0 / np.sqrt(D)
        return {'h_target': jax.random.normal(ks[0], (BT, D), jnp.float32), 'h_neigh': jax.random.normal(ks[1], (BN, D), jnp.float32), 'adjacency': jax.random.randint(ks[2], (BT, BN), 0, 2, jnp.int32), 'edge_types': jax.random.randint(ks[3], (BT, BN), 0, 2, jnp.int32), 'Wq': jax.random.normal(ks[4], (D, D), jnp.float32) * s, 'bq': jnp.zeros((D,), jnp.float32), 'Wk': jax.random.normal(ks[5], (D, D), jnp.float32) * s, 'bk': jnp.zeros((D,), jnp.float32), 'Wv': jax.random.normal(ks[6], (D, D), jnp.float32) * s, 'bv': jnp.zeros((D,), jnp.float32), 'Wo': jax.random.normal(ks[7], (D, D), jnp.float32) * s, 'bo': jnp.zeros((D,), jnp.float32), 'E': jax.random.normal(ks[8], (2, D), jnp.float32)}
    _L0_gnn_all = _L0_gnn_setup()
    _L0_gnn_in = {k: v for k, v in _L0_gnn_all.items() if k in ('h_neigh', 'Wq', 'bq', 'Wk', 'bk', 'Wv', 'bv', 'Wo', 'bo', 'E')}
    del _L0_gnn_all

    def _L0_ffn_setup():
        import jax, jax.numpy as jnp
        import numpy as np
        C = 128
        HID = 512
        E = 8
        TEMP = 1.0
        key = jax.random.key(seed)
        ks = jax.random.split(key, 7)
        x = jax.random.normal(ks[0], (8, 8192, C), dtype=jnp.float32)
        W1 = jax.random.normal(ks[1], (C, HID), dtype=jnp.float32) * 0.02
        b1 = jnp.zeros((HID,), dtype=jnp.float32)
        Wg = jax.random.normal(ks[2], (HID, E), dtype=jnp.float32) * 0.02
        bg = jnp.zeros((E,), dtype=jnp.float32)
        Wd = jax.random.normal(ks[3], (E, HID, C), dtype=jnp.float32) * 0.02
        bd = jnp.zeros((E, C), dtype=jnp.float32)
        return {'x': x, 'W1': W1, 'b1': b1, 'Wg': Wg, 'bg': bg, 'Wd': Wd, 'bd': bd}
    _L0_ffn_all = _L0_ffn_setup()
    _L0_ffn_in = {k: v for k, v in _L0_ffn_all.items() if k in ('W1', 'b1', 'Wg', 'bg', 'Wd', 'bd')}
    del _L0_ffn_all

    def _L1_gnn_setup():
        import jax, jax.numpy as jnp
        import numpy as np
        N, D, H = (4096, 128, 128)
        KEEP_RATIO = 0.5
        TEMP = 1.0
        COS_EPS = 0.0001
        NEG = -9000000000000000.0

        def _cos_normalize(x):
            n = jnp.linalg.norm(x, axis=-1, keepdims=True)
            return x / jnp.maximum(n, COS_EPS)
        key = jax.random.key(seed)
        k1, k2, k3, k4 = jax.random.split(key, 4)
        features = jax.random.normal(k1, (N, D), dtype=jnp.float32)
        adj = jax.random.randint(k2, (N, N), 0, 2, dtype=jnp.int32)
        Wq = jax.random.normal(k3, (H, D), dtype=jnp.float32) * 0.001
        Wk = jax.random.normal(k4, (H, D), dtype=jnp.float32) * 0.001
        return {'features': features, 'adj': adj, 'Wq': Wq, 'Wk': Wk}
    _L1_gnn_all = _L1_gnn_setup()
    _L1_gnn_in = {k: v for k, v in _L1_gnn_all.items() if k in ('Wq', 'Wk')}
    del _L1_gnn_all

    def _L1_ffn_setup():
        import jax, jax.numpy as jnp
        import numpy as np
        TOP_K = 2
        key = jax.random.key(seed)
        ks = jax.random.split(key, 4)
        B, L, D, H, E = (8, 2048, 128, 512, 8)
        s = 0.02
        return {'x': jax.random.normal(ks[0], (B, L, D), jnp.float32), 'Wg': jax.random.normal(ks[1], (D, E), jnp.float32) * s, 'bg': jnp.zeros((E,), jnp.float32), 'W1': jax.random.normal(ks[2], (E, D, H), jnp.float32) * s, 'b1': jnp.zeros((E, H), jnp.float32), 'W2': jax.random.normal(ks[3], (E, H, D), jnp.float32) * s, 'b2': jnp.zeros((E, D), jnp.float32)}
    _L1_ffn_all = _L1_ffn_setup()
    _L1_ffn_in = {k: v for k, v in _L1_ffn_all.items() if k in ('Wg', 'bg', 'W1', 'b1', 'W2', 'b2')}
    del _L1_ffn_all
    return {'x': x, 'adj': adj, 'L0_gnn_h_neigh': _L0_gnn_in['h_neigh'], 'L0_gnn_Wq': _L0_gnn_in['Wq'], 'L0_gnn_bq': _L0_gnn_in['bq'], 'L0_gnn_Wk': _L0_gnn_in['Wk'], 'L0_gnn_bk': _L0_gnn_in['bk'], 'L0_gnn_Wv': _L0_gnn_in['Wv'], 'L0_gnn_bv': _L0_gnn_in['bv'], 'L0_gnn_Wo': _L0_gnn_in['Wo'], 'L0_gnn_bo': _L0_gnn_in['bo'], 'L0_gnn_E': _L0_gnn_in['E'], 'L0_ffn_W1': _L0_ffn_in['W1'], 'L0_ffn_b1': _L0_ffn_in['b1'], 'L0_ffn_Wg': _L0_ffn_in['Wg'], 'L0_ffn_bg': _L0_ffn_in['bg'], 'L0_ffn_Wd': _L0_ffn_in['Wd'], 'L0_ffn_bd': _L0_ffn_in['bd'], 'L1_gnn_Wq': _L1_gnn_in['Wq'], 'L1_gnn_Wk': _L1_gnn_in['Wk'], 'L1_ffn_Wg': _L1_ffn_in['Wg'], 'L1_ffn_bg': _L1_ffn_in['bg'], 'L1_ffn_W1': _L1_ffn_in['W1'], 'L1_ffn_b1': _L1_ffn_in['b1'], 'L1_ffn_W2': _L1_ffn_in['W2'], 'L1_ffn_b2': _L1_ffn_in['b2']}

def reference(x, adj, L0_gnn_h_neigh, L0_gnn_Wq, L0_gnn_bq, L0_gnn_Wk, L0_gnn_bk, L0_gnn_Wv, L0_gnn_bv, L0_gnn_Wo, L0_gnn_bo, L0_gnn_E, L0_ffn_W1, L0_ffn_b1, L0_ffn_Wg, L0_ffn_bg, L0_ffn_Wd, L0_ffn_bd, L1_gnn_Wq, L1_gnn_Wk, L1_ffn_Wg, L1_ffn_bg, L1_ffn_W1, L1_ffn_b1, L1_ffn_W2, L1_ffn_b2):
    import jax
    import jax.numpy as jnp

    def _L0_gnn_ref(h_target, h_neigh, adjacency, edge_types, Wq, bq, Wk, bk, Wv, bv, Wo, bo, E):
        import jax, jax.numpy as jnp
        import numpy as np
        BT, BN, D, H = (512, 512, 128, 8)
        DH = D // H
        Bt, d = h_target.shape
        Bn = h_neigh.shape[0]
        msg = h_neigh[None, :, :] + E[edge_types]
        q = (h_target @ Wq.T + bq).reshape(Bt, H, DH)
        k = (msg @ Wk.T + bk).reshape(Bt, Bn, H, DH)
        v = (msg @ Wv.T + bv).reshape(Bt, Bn, H, DH)
        scores = jnp.einsum('bhd,bnhd->bhn', q, k) / np.sqrt(DH).astype(np.float32)
        mask = adjacency[:, None, :] == 0
        scores = jnp.where(mask, jnp.float32(-1000000000.0), scores)
        attn = jax.nn.softmax(scores, axis=-1)
        attn = jnp.where(mask, jnp.float32(0.0), attn)
        out = jnp.einsum('bhn,bnhd->bhd', attn, v).reshape(Bt, d)
        return out @ Wo.T + bo

    def _L0_ffn_ref(x, W1, b1, Wg, bg, Wd, bd):
        import jax, jax.numpy as jnp
        import numpy as np
        C = 128
        HID = 512
        E = 8
        TEMP = 1.0
        orig_shape = x.shape
        xf = x.reshape(-1, orig_shape[-1])
        H = jax.nn.gelu(xf @ W1 + b1, approximate=False)
        probs = jax.nn.softmax((H @ Wg + bg) / TEMP, axis=-1)
        assign = jnp.argmax(probs, axis=-1)
        out = jnp.zeros_like(xf)
        for e in range(Wd.shape[0]):
            y = H @ Wd[e] + bd[e]
            sel = (assign == e)[:, None]
            out = out + jnp.where(sel, probs[:, e:e + 1] * y, 0.0)
        return out.reshape(orig_shape)

    def _L1_gnn_ref(features, adj, Wq, Wk):
        import jax, jax.numpy as jnp
        import numpy as np
        N, D, H = (4096, 128, 128)
        KEEP_RATIO = 0.5
        TEMP = 1.0
        COS_EPS = 0.0001
        NEG = -9000000000000000.0

        def _cos_normalize(x):
            n = jnp.linalg.norm(x, axis=-1, keepdims=True)
            return x / jnp.maximum(n, COS_EPS)
        Qn = _cos_normalize(features @ Wq.T)
        Kn = _cos_normalize(features @ Wk.T)
        raw_att = Kn @ Qn.T
        att = jnp.where(adj > 0, raw_att, NEG) * TEMP
        att = jax.nn.softmax(att, axis=1)
        prop_fea = att @ features
        adj_mask = (jnp.sum(adj, axis=1) > 0).astype(features.dtype)[:, None]
        prop_fea = adj_mask * prop_fea + (1.0 - adj_mask) * features
        return (1.0 - KEEP_RATIO) * prop_fea + KEEP_RATIO * features

    def _L1_ffn_ref(x, Wg, bg, W1, b1, W2, b2):
        import jax, jax.numpy as jnp
        import numpy as np
        TOP_K = 2
        B, L, D = x.shape
        E = W1.shape[0]
        xf = x.reshape(-1, D)
        gate_logits = xf @ Wg + bg
        top_w, top_i = jax.lax.top_k(gate_logits, TOP_K)
        top_w = jax.nn.softmax(top_w, axis=-1)
        w_dense = jnp.sum(jax.nn.one_hot(top_i, E, dtype=xf.dtype) * top_w[..., None], axis=1)
        out = jnp.zeros_like(xf)
        for e in range(E):
            h = jax.nn.gelu(xf @ W1[e] + b1[e], approximate=False)
            out = out + w_dense[:, e:e + 1] * (h @ W2[e] + b2[e])
        return out.reshape(B, L, D)
    x = x + _L0_gnn_ref(_layernorm(x, axis=-1), L0_gnn_h_neigh, adj, adj, L0_gnn_Wq, L0_gnn_bq, L0_gnn_Wk, L0_gnn_bk, L0_gnn_Wv, L0_gnn_bv, L0_gnn_Wo, L0_gnn_bo, L0_gnn_E)
    x = x + _L0_ffn_ref(_layernorm(x, axis=-1)[None], L0_ffn_W1, L0_ffn_b1, L0_ffn_Wg, L0_ffn_bg, L0_ffn_Wd, L0_ffn_bd)[0]
    x = x + _L1_gnn_ref(_layernorm(x, axis=-1), adj, L1_gnn_Wq, L1_gnn_Wk)
    x = x + _L1_ffn_ref(_layernorm(x, axis=-1)[None], L1_ffn_Wg, L1_ffn_bg, L1_ffn_W1, L1_ffn_b1, L1_ffn_W2, L1_ffn_b2)[0]
    return x

_drawn_inputs = setup_inputs


def setup_inputs(seed=0):
    import zlib

    import numpy as np

    out = dict(_drawn_inputs(seed))
    spreads = {'L0_gnn_bq': (0.0, 0.461),
     'L0_gnn_bk': (0.0, 2.0),
     'L0_gnn_bv': (0.0, 0.1),
     'L0_gnn_bo': (0.0, 0.1),
     'L0_ffn_b1': (0.0, 0.8),
     'L0_ffn_bg': (0.0, 0.608),
     'L0_ffn_bd': (0.0, 0.8),
     'L1_ffn_bg': (0.0, 0.334),
     'L1_ffn_b1': (0.0, 0.8),
     'L1_ffn_b2': (0.0, 0.548)}
    factors = {'L0_ffn_W1': 8.0,
     'L0_ffn_Wg': 7.129,
     'L0_ffn_Wd': 8.0,
     'L1_gnn_Wq': 64.0,
     'L1_gnn_Wk': 64.0,
     'L1_ffn_W1': 3.45,
     'L1_ffn_W2': 3.19}
    for name, (base, spread) in spreads.items():
        noise = np.random.default_rng([zlib.crc32(name.encode()), seed]).standard_normal(out[name].shape)
        drawn = base * np.exp(spread * noise) if base else spread * noise
        out[name] = jnp.asarray(drawn.astype(out[name].dtype))
    for name, factor in factors.items():
        out[name] = (out[name] * factor).astype(out[name].dtype)
    return out
```

```python
from contextlib import ExitStack

import concourse.bass as bass
from concourse import mybir

F32 = mybir.dt.float32
F32R = mybir.dt.float32r
BF16 = mybir.dt.bfloat16
I32 = mybir.dt.int32
U32 = mybir.dt.uint32
ALU = mybir.AluOpType
ACT = mybir.ActivationFunctionType
AX = mybir.AxisListType.X

P = 128
N = 512
T = N // P
D = 128
H = 8
DH = D // H
PAIRS = H // 2
GROUPS = H // 4
HID = 512
KT = HID // P
E = 8
EH = E // 2
LN_EPS = 1e-5
COS_EPS = 1e-4
MASKED = -(2.0 ** 100)
LEAST_MAX = -(2.0 ** 60)
LEAST_SUM = 1e-30

BLOCK = 32
ONES_COL = DH
EARLY = {}
LATE = {}


def _place(table, sizes):
    at = 0
    for name, size in sizes:
        table[name] = (at, at + size)
        at += size
    return at


N_EARLY = _place(EARLY, [("ident", P), ("e1", 1), ("bq", PAIRS), ("bk", H), ("hb1", KT), ("fb1", E * KT),
                         ("hnT", N), ("wk", H * P), ("wv", 2 * P), ("wq", PAIRS * P)])
N_LATE = _place(LATE, [("wo", D), ("w1", HID), ("wg0", KT * E), ("wkq", 2 * D), ("wg1", E), ("sel", E * P)])
ROWS = {}
N_ROWS = _place(ROWS, [("bv", 2 * P), ("bo", D), ("bg0", E), ("bg1", E), ("iota", E)])

N_CHUNKS = 2 * KT + 2 * E
WD_CHUNKS = 2 * KT
PRELOADED = WD_CHUNKS + 4
SLOTS = 12
STAGES = 4


POWERS = [("ln1", T), ("ln2", T), ("f0", 1), ("f1", 1), ("c0", 2), ("f2", 1), ("c1", 2), ("f3", 1), ("c2", 2),
          ("c3", 2), ("ln4", T)]
POWER = {}
N_POWERS = _place(POWER, POWERS)
POWER_NO = {name: i for i, (name, _) in enumerate(POWERS)}


def build(nc, x, adj, early, late, rows, biases, chunks, out):
    with ExitStack() as ctx:
        def sb(name, shape, dt=F32):
            return ctx.enter_context(nc.sbuf_tensor(name, shape, dt))

        def sem(name):
            return ctx.enter_context(nc.semaphore(name))

        ps = ctx.enter_context(nc.psum_tensor("ps", [P, 8, 512], F32))

        x_sb = sb("x_sb", [P, T, D])
        early_sb = sb("early_sb", [P, N_EARLY])
        late_sb = sb("late_sb", [P, N_LATE])
        rows_sb = sb("rows_sb", [P, N_ROWS])
        bias_sb = sb("bias_sb", [E, 2 * D])
        stage = sb("stage", [P, STAGES, 512])
        adj_sb = stage[:, :, :].bitcast(I32)
        w_hi = sb("w_hi", [P, SLOTS, 512], F32R)
        w_lo = sb("w_lo", [P, SLOTS, 512], F32R)
        mask = sb("mask", [P, T, N], BF16)
        maskT = sb("maskT", [P, T, N], BF16)
        identb = sb("identb", [P, P], BF16)
        sel = sb("sel", [P, E, P], F32R)
        msgT = sb("msgT", [P, N])
        k_st = sb("k_st", [P, H, N], F32R)
        q_st = sb("q_st", [P, PAIRS, N], F32R)
        v_sb = sb("v_sb", [P, T, 2 * P])
        big = sb("big", [P, 16, 512])
        h_hi = sb("h_hi", [P, KT, 512], F32R)
        h_lo = sb("h_lo", [P, KT, 512], F32R)
        xbo = sb("xbo", [P, T, D])
        x1 = sb("x1", [P, T, D])
        x2 = sb("x2", [P, T, D])
        x3 = sb("x3", [P, T, D])
        xf = sb("xf", [P, T, D])
        f_sb = sb("f_sb", [P, T, D + 2])
        xn = sb("xn", [P, T, D])
        xT = sb("xT", [P, N])
        xT_hi = sb("xT_hi", [P, N], F32R)
        xT_lo = sb("xT_lo", [P, N], F32R)
        attn = sb("attn", [P, T, D])
        o_sb = sb("o_sb", [P, N])
        acc = o_sb
        part = sb("part", [P, 2, N])
        squares = sb("squares", [P, 2 * T, D], BF16)
        stats = sb("stats", [P, T, 6])
        mv = sb("mv", [P, T, 2])
        base = sb("base", [P, N_POWERS])
        root = sb("root", [P, N_POWERS])
        minus_half = sb("minus_half", [P, T])
        mx = sb("mx", [P, T, H])
        negm = sb("negm", [P, T, P])
        den = sb("den", [P, 2 * H])
        rec = sb("rec", [P, 2 * H])
        logit = sb("logit", [P, T, E])
        top = sb("top", [P, T, E])
        topi = sb("topi", [P, T, E], U32)
        topf = sb("topf", [P, T, E])
        prob = sb("prob", [P, T, E])
        psum_ = sb("psum_", [P, T])
        gate = sb("gate", [P, T, 64])
        gateT = sb("gateT", [E, N])
        wT_st = sb("wT_st", [P, N], F32R)
        w01 = sb("w01", [P, T, 2])
        oh = sb("oh", [P, T, E])
        ss = sb("ss", [P, T, 2])
        prec = sb("prec", [P, T])
        lone = sb("lone", [P, T])

        hf = big[:, 0:KT, :]
        prob2 = big[:, 0:T, :]
        kqn = big[:, 4:6, :].rearrange("p a (b c) -> p (a b) c", c=2 * D)
        kqT = big[:, 6:8, :]
        wb = big[:, 8:16, :]

        def e_(name, i=0, n=1):
            a, b = EARLY[name]
            w = (b - a) // n
            return early_sb[:, a + i * w:a + (i + 1) * w]

        def l_(name, i=0, n=1):
            a, b = LATE[name]
            w = (b - a) // n
            return late_sb[:, a + i * w:a + (i + 1) * w]

        def r_(name):
            return rows_sb[:, ROWS[name][0]:ROWS[name][1]]

        def tok(t):
            return slice(t * P, (t + 1) * P)

        ident = e_("ident")

        names = """ld_x ld_early ld_adj ld_late ld_rows ld_bias st_out
            mask_made msg_made identb_made sel_made ln1 ln2 ln4 fr
            k_mm k_hi k_lo v_mm v_made xT1_tr xT1 q_mm q_hi q_lo mt_tr mt_made
            sa rowmax negm_made nm_tr nm_in sb_mm exp1 pv1 o_copied o_tr o_normed
            at_tr at_copied op_mm x1_made xT2_tr xT2 h0_mm h0_act h0_hi h0_lo lg0_mm lg0_shift lg0_exp gate0
            g0_tr g0_copied bd_mm gm2 combined x2_made
            f_tr f_copied kq_mm kq_ss kq_normed kq_tr kq_copied at2_mm exp2 pv2 x3_made
            xT4_tr xT4_hi xT4_lo xT4 h_mm h_act h_hi_s h_lo_s y_mm lg1_mm lg1_d lg1_tanh gate1
            w_tr w_st wb_mm wb_made part_made acc_made fin_mm out_made
            power_in power_out split wd_free w1_free w2_free chain_v chain_g pool_chain zeroed""".split()
        S = {n: sem(n) for n in names}
        ld_stage = [sem(f"ld_stage{i}") for i in range(STAGES)]

        block = ctx.enter_context(nc.Block())

        def chunk_free(eng, c):
            old = c - SLOTS
            if old < 0:
                return
            if old < WD_CHUNKS:
                eng.wait_ge(S["gm2"], T)
            elif (old - WD_CHUNKS) % 2 == 0:
                eng.wait_ge(S["h_mm"], KT * ((old - WD_CHUNKS) // 2 + 1))
            else:
                eng.wait_ge(S["y_mm"], (old - WD_CHUNKS) // 2 + 1)

        @block.sync
        def _(sp):
            sp.dma_start(x_sb[:, :, :], x.rearrange("(t p) d -> p t d", p=P)).then_inc(S["ld_x"], 16)
            sp.dma_start(early_sb[:, :], early).then_inc(S["ld_early"], 16)
            sp.dma_start(late_sb[:, :], late).then_inc(S["ld_late"], 16)
            sp.dma_start(bias_sb[:, :], biases).then_inc(S["ld_bias"], 16)
            sp.wait_ge(S["mask_made"], 1)
            for c in range(N_CHUNKS):
                if c >= STAGES:
                    sp.wait_ge(S["split"], c - STAGES + 1)
                sp.dma_start(stage[:, c % STAGES, :], chunks[c]).then_inc(ld_stage[c % STAGES], 16)

        @block.gpsimd
        def _(pool):
            nc.gpsimd.memset(minus_half[:, :], -0.5)
            nc.gpsimd.memset(negm[:, :, :], 0.0)
            nc.gpsimd.memset(f_sb[:, :, D:D + 1], 1.0)
            nc.gpsimd.memset(f_sb[:, :, D + 1:D + 2], 0.0)
            nc.gpsimd.memset(gate[:, :, :], 0.0)
            nc.gpsimd.memset(wT_st[:, :].bitcast(F32), 0.0).then_inc(S["zeroed"], 1)

            def power(name):
                a, b = POWER[name]
                pool.wait_ge(S["power_in"], POWER_NO[name] + 1)
                nc.gpsimd.tensor_tensor(root[:, a:b], base[:, a:b], minus_half[:, 0:b - a], ALU.pow)\
                    .then_inc(S["power_out"], 1)

            def split(c):
                pool.wait_ge(ld_stage[c % STAGES], 16 * (c // STAGES + 1))
                chunk_free(pool, c)
                raw, hi, lo = stage[:, c % STAGES, :], w_hi[:, c % SLOTS, :], w_lo[:, c % SLOTS, :]
                nc.gpsimd.tensor_scalar(hi, raw, 1.0, 0.0, ALU.mult, ALU.add).then_inc(S["pool_chain"], 1)
                pool.wait_ge(S["pool_chain"], c + 1)
                nc.gpsimd.tensor_tensor(lo, raw, hi, ALU.subtract).then_inc(S["split"], 1)

            pool.wait_ge(S["zeroed"], 1)
            power("ln1")
            pool.wait_ge(S["ld_adj"], 16)
            nc.gpsimd.tensor_scalar(mask[:, :, :], adj_sb, 0.0, MASKED, ALU.is_equal, ALU.mult)\
                .then_inc(S["mask_made"], 1)
            for c in range(PRELOADED):
                split(c)
            for name, _ in POWERS[1:-1]:
                power(name)
            for c in range(PRELOADED, PRELOADED + 4):
                split(c)
            power("ln4")
            for e in range(E - 1):
                if PRELOADED + 4 + 2 * e < N_CHUNKS:
                    split(PRELOADED + 4 + 2 * e)
                    split(PRELOADED + 4 + 2 * e + 1)
                if e >= 1:
                    pool.wait_ge(S["part_made"], e + 1)
                    pool.wait_ge(S["acc_made"], e)
                    nc.gpsimd.tensor_tensor(acc[:, :], acc[:, :], part[:, e % 2, :], ALU.add)\
                        .then_inc(S["acc_made"], 1)

        @block.scalar
        def _(act):
            act.dma_start(adj_sb, adj.rearrange("(t p) n -> p t n", p=P)).then_inc(S["ld_adj"], 16)
            act.dma_start(rows_sb[:, :], rows.partition_broadcast(P)).then_inc(S["ld_rows"], 16)

            act.wait_ge(S["ld_early"], 16)
            for h in range(H):
                act.wait_ge(S["k_mm"], h + 1)
                nc.scalar.activation(k_st[:, h, :], ps[:, h % 2, :], ACT.Identity,
                                     bias=e_("bk", h, H)).then_inc(S["k_hi"], 1)
            act.wait_ge(S["xT1_tr"], 1)
            nc.scalar.copy(xT[:, :], ps[:, 4, :]).then_inc(S["xT1"], 1)
            for p in range(PAIRS):
                act.wait_ge(S["q_mm"], p + 1)
                nc.scalar.activation(q_st[:, p, :], ps[:, p % 2, :], ACT.Identity,
                                     bias=e_("bq", p, PAIRS)).then_inc(S["q_hi"], 1)
            for t in range(T):
                act.wait_ge(S["mt_tr"], t + 1)
                nc.scalar.copy(maskT[:, t, :], ps[:, 4 + t, 0:256].bitcast(BF16)).then_inc(S["mt_made"], 1)

            for h in range(H):
                if h == 4:
                    act.wait_ge(S["pv1"], 1)
                    nc.scalar.copy(o_sb[:, :], ps[:, 7, :]).then_inc(S["o_copied"], 1)
                for half in range(2):
                    i = 2 * h + half
                    b = 2 + 2 * (i % 2)
                    act.wait_ge(S["sb_mm"], i + 1)
                    nc.scalar.activation(big[:, 4 * (h % 4) + 2 * half:4 * (h % 4) + 2 * half + 2, :],
                                         ps[:, b:b + 2, :], ACT.Exp, scale=DH ** -0.5).then_inc(S["exp1"], 1)
            act.wait_ge(S["pv1"], 2)
            act.wait_ge(S["o_tr"], 1)
            nc.scalar.copy(o_sb[:, :], ps[:, 7, :]).then_inc(S["o_copied"], 1)
            act.wait_ge(S["at_tr"], 1)
            nc.scalar.copy(xT[:, :], ps[:, 0, :]).then_inc(S["at_copied"], 1)
            act.wait_ge(S["xT2_tr"], 1)
            nc.scalar.copy(xT[:, :], ps[:, 2, :]).then_inc(S["xT2"], 1)

            for c in range(KT):
                act.wait_ge(S["h0_mm"], c + 1)
                nc.scalar.activation(hf[:, c, :], ps[:, 3 + c, :], ACT.Gelu,
                                     bias=e_("hb1", c, KT)).then_inc(S["h0_act"], 1)
            act.wait_ge(S["lg0_shift"], 1)
            nc.scalar.activation(prob[:, :, :], prob[:, :, :], ACT.Exp).then_inc(S["lg0_exp"], 1)

            for t in range(T):
                act.wait_ge(S["f_tr"], t + 1)
                nc.scalar.copy(xT[:, tok(t)], ps[:, 4, 0:P]).then_inc(S["f_copied"], 1)
                act.wait_ge(S["kq_mm"], t + 1)
                for i in range(2):
                    last = nc.scalar.activation(squares[:, 2 * t + i, :], ps[:, 5, i * D:(i + 1) * D], ACT.Square,
                                                accum_out=ss[:, t, i:i + 1])
                last.then_inc(S["kq_ss"], 1)
                act.wait_ge(S["kq_tr"], t + 1)
                nc.scalar.copy(kqT[:, :, tok(t)], ps[:, 6, 0:2 * P].rearrange("p (a b) -> p a b", a=2))\
                    .then_inc(S["kq_copied"], 1)
            for j in range(T):
                act.wait_ge(S["at2_mm"], j + 1)
                nc.scalar.activation(prob2[:, j, :], ps[:, j, :], ACT.Exp).then_inc(S["exp2"], 1)
            act.wait_ge(S["xT4_tr"], 1)
            nc.scalar.copy(xT_hi[:, :], ps[:, 0, :]).then_inc(S["xT4_hi"], 1)
            act.wait_ge(S["xT4_lo"], 1)
            nc.scalar.copy(xT[:, :], ps[:, 0, :]).then_inc(S["xT4"], 1)

            def hidden(e):
                for c in range(KT):
                    i = e * KT + c
                    act.wait_ge(S["h_mm"], i + 1)
                    if i >= KT:
                        act.wait_ge(S["h_lo_s"], i - KT + 1)
                    nc.scalar.activation(hf[:, c, :], ps[:, (c + 1) % 4, :], ACT.Gelu,
                                         bias=e_("fb1", i, E * KT)).then_inc(S["h_act"], 1)

            def broadcast_copy(e):
                act.wait_ge(S["wb_mm"], e + 1)
                nc.scalar.copy(wb[:, e, :], ps[:, 6 + e % 2, :]).then_inc(S["wb_made"], 1)

            for e in range(E):
                hidden(e)
                if e == 0:
                    act.wait_ge(S["lg1_d"], 1)
                    nc.scalar.activation(psum_[:, :], psum_[:, :], ACT.Tanh, scale=0.5).then_inc(S["lg1_tanh"], 1)
                else:
                    broadcast_copy(e - 1)
            broadcast_copy(E - 1)

            for t in range(T):
                act.wait_ge(S["out_made"], t + 1)
                act.dma_start(out[tok(t), :], x3[:, t, :]).then_inc(S["st_out"], 16)
            act.wait_ge(S["st_out"], 16 * T)

        @block.vector
        def _(dve):
            steps = {"n": 0}

            def then(ins):
                steps["n"] += 1
                ins.then_inc(S["chain_v"], 1)
                dve.wait_ge(S["chain_v"], steps["n"])

            def power(name):
                dve.wait_ge(S["power_out"], POWER_NO[name] + 1)
                return root[:, POWER[name][0]:POWER[name][1]]

            def layer_norm(src, dst, tiles, name, done):
                for t in tiles:
                    last = nc.vector.bn_stats(out=stats[:, t, :], in_=src[:, t, :])
                then(last)
                for t in tiles:
                    last = nc.vector.bn_aggr(out=mv[:, t, :], in_=stats[:, t, :])
                then(last)
                a, b = POWER[name]
                nc.vector.tensor_scalar(base[:, a:b], mv[:, tiles[0]:tiles[-1] + 1, 1], LN_EPS, None, ALU.add)\
                    .then_inc(S["power_in"], 1)
                rstd = power(name)
                for i, t in enumerate(tiles):
                    nc.vector.tensor_scalar(dst[:, t, 0:D], src[:, t, :], mv[:, t, 0:1], rstd[:, i:i + 1],
                                            ALU.subtract, ALU.mult).then_inc(done, 1)

            dve.wait_ge(S["ld_x"], 16)
            layer_norm(x_sb, xn, range(T), "ln1", S["ln1"])
            dve.wait_ge(S["ld_early"], 16)
            nc.vector.tensor_scalar(msgT[:, :], e_("hnT"), e_("e1"), None, ALU.add).then_inc(S["msg_made"], 1)
            nc.vector.tensor_copy(identb[:, :], ident).then_inc(S["identb_made"], 1)
            for h in range(H):
                dve.wait_ge(S["k_hi"], h + 1)
                b = slice(BLOCK, 2 * BLOCK)
                nc.vector.scalar_tensor_tensor(out=k_st[b, h, :], in0=ps[b, h % 2, :], scalar=e_("bk", h, H)[b, :],
                                               in1=k_st[b, h, :], op0=ALU.add, op1=ALU.subtract)\
                    .then_inc(S["k_lo"], 1)
            dve.wait_ge(S["ld_rows"], 16)
            for i in range(2):
                dve.wait_ge(S["v_mm"], i + 1)
                nc.vector.tensor_tensor(v_sb[:, 2 * i:2 * i + 2, :],
                                        ps[:, 2 + i, :].rearrange("p (a b) -> p a b", a=2),
                                        r_("bv").unsqueeze(1).to_broadcast([P, 2, 2 * P]), ALU.add)\
                    .then_inc(S["v_made"], 1)
            for p in range(PAIRS):
                dve.wait_ge(S["q_hi"], p + 1)
                b = slice(2 * BLOCK, 3 * BLOCK)
                nc.vector.scalar_tensor_tensor(out=q_st[b, p, :], in0=ps[b, p % 2, :],
                                               scalar=e_("bq", p, PAIRS)[b, :], in1=q_st[b, p, :],
                                               op0=ALU.add, op1=ALU.subtract).then_inc(S["q_lo"], 1)
            dve.wait_ge(S["mask_made"], 1)
            dve.wait_ge(S["zeroed"], 1)

            def row_max(p):
                for i in range(2 * T):
                    a, t = divmod(i, T)
                    n = p * 2 * T + i
                    dve.wait_ge(S["sa"], n + 1)
                    nc.vector.tensor_tensor_reduce(out=ps[:, n % 2, :], in0=ps[:, n % 2, :], in1=mask[:, t, :],
                                                   scale=1.0, scalar=-3e38, op0=ALU.add, op1=ALU.max,
                                                   accum_out=mx[:, t, 2 * p + a:2 * p + a + 1])\
                        .then_inc(S["rowmax"], 1)
                dve.wait_ge(S["rowmax"], (p + 1) * 2 * T)
                c = 3 * BLOCK + 2 * p
                nc.vector.tensor_scalar(negm[:, :, c:c + 2], mx[:, :, 2 * p:2 * p + 2], LEAST_MAX, -1.0,
                                        ALU.max, ALU.mult).then_inc(S["negm_made"], 1)
                dve.wait_ge(S["nm_tr"], p + 1)
                b = slice(3 * BLOCK, 4 * BLOCK)
                nc.vector.tensor_copy(q_st[b, p, :], ps[b, 6, :]).then_inc(S["nm_in"], 1)

            def normalise(g):
                dve.wait_ge(S["o_tr"], g + 1)
                o = ps[:, 7, :].rearrange("p (th c) -> p th c", c=BLOCK)
                then(nc.vector.tensor_scalar(den[:, :], o[:, :, ONES_COL], LEAST_SUM, None, ALU.max))
                then(nc.vector.reciprocal(rec[:, :], den[:, :]))
                for t in range(T):
                    last = nc.vector.tensor_tensor(
                        attn[:, t, g * 64:(g + 1) * 64].rearrange("p (h d) -> p h d", d=DH),
                        o[:, 4 * t:4 * t + 4, 0:DH],
                        rec[:, 4 * t:4 * t + 4].unsqueeze(2).to_broadcast([P, 4, DH]), ALU.mult)
                last.then_inc(S["o_normed"], 1)

            for p in range(PAIRS):
                row_max(p)
                if p == 0:
                    nc.vector.tensor_tensor(xbo[:, :, :], x_sb[:, :, :],
                                            r_("bo").unsqueeze(1).to_broadcast([P, T, D]), ALU.add)
                    dve.wait_ge(S["ld_late"], 16)
                    nc.vector.tensor_copy(sel[:, :, :], l_("sel").rearrange("p (e m) -> p e m", e=E))\
                        .then_inc(S["sel_made"], 1)
            normalise(0)
            normalise(1)
            dve.wait_ge(S["op_mm"], 1)
            nc.vector.tensor_tensor(x1[:, :, :], ps[:, 1, :].rearrange("p (t d) -> p t d", t=T), xbo[:, :, :],
                                    ALU.add).then_inc(S["x1_made"], 1)
            dve.wait_ge(S["x1_made"], 1)
            layer_norm(x1, xn, range(T), "ln2", S["ln2"])

            for c in range(KT):
                dve.wait_ge(S["h0_act"], c + 1)
                nc.vector.tensor_copy(h_hi[:, c, :], hf[:, c, :]).then_inc(S["h0_hi"], 1)
                dve.wait_ge(S["h0_hi"], c + 1)
                nc.vector.tensor_tensor(h_lo[:, c, :], hf[:, c, :], h_hi[:, c, :], ALU.subtract)\
                    .then_inc(S["h0_lo"], 1)

            def logits_top(bank, bias, mm):
                dve.wait_ge(mm, 1)
                then(nc.vector.tensor_tensor(logit[:, :, :], ps[:, bank, 0:T * E].rearrange("p (t e) -> p t e", t=T),
                                             bias.unsqueeze(1).to_broadcast([P, T, E]), ALU.add))
                for t in range(T):
                    last = nc.vector.max(out=top[:, t, :], in_=logit[:, t, :])
                then(last)

            def top_numbers():
                for t in range(T):
                    last = nc.vector.max_index(out=topi[:, t, :], in_max=top[:, t, :], in_values=logit[:, t, :])
                then(last)
                then(nc.vector.tensor_copy(topf[:, :, :], topi[:, :, :]))

            logits_top(7, r_("bg0"), S["lg0_mm"])
            nc.vector.tensor_tensor(prob[:, :, :], logit[:, :, :], top[:, :, 0:1].to_broadcast([P, T, E]),
                                    ALU.subtract).then_inc(S["lg0_shift"], 1)
            top_numbers()
            dve.wait_ge(S["lg0_exp"], 1)
            then(nc.vector.tensor_reduce(psum_[:, :], prob[:, :, :], AX, ALU.add))
            then(nc.vector.reciprocal(prec[:, :], psum_[:, :]))
            for t in range(T):
                last = nc.vector.tensor_scalar(gate[:, t, 0:E], r_("iota"), topf[:, t, 0:1], prec[:, t:t + 1],
                                               ALU.is_equal, ALU.mult)
            last.then_inc(S["gate0"], 1)
            dve.wait_ge(S["gate0"], 1)
            dve.wait_ge(S["g0_tr"], 1)
            nc.vector.tensor_copy(gateT[:, :], ps[0:E, 6, :]).then_inc(S["g0_copied"], 1)

            def combine(t):
                dve.wait_ge(S["gm2"], t + 1)
                b = 2 * (t % 2)
                for e in range(E):
                    ins = nc.vector.scalar_tensor_tensor(
                        out=x2[:, t, :], in0=ps[:, b + e // EH, (e % EH) * D:(e % EH + 1) * D],
                        scalar=gate[:, t, e:e + 1], in1=(x1 if e == 0 else x2)[:, t, :],
                        op0=ALU.mult, op1=ALU.add)
                    if e < E - 1:
                        then(ins)
                ins.then_inc(S["combined"], 1)
                dve.wait_ge(S["combined"], t + 1)
                dve.wait_ge(S["bd_mm"], 1)
                nc.vector.tensor_tensor(x2[:, t, :], x2[:, t, :], ps[:, 7, tok(t)], ALU.add)\
                    .then_inc(S["x2_made"], 1)
                dve.wait_ge(S["x2_made"], t + 1)

            def cosines(t):
                dve.wait_ge(S["kq_ss"], t + 1)
                a, b = POWER[f"c{t}"]
                nc.vector.tensor_scalar(base[:, a:b], ss[:, t, :], COS_EPS ** 2, None, ALU.max)\
                    .then_inc(S["power_in"], 1)
                rs = power(f"c{t}")
                for i in range(2):
                    last = nc.vector.tensor_scalar(kqn[:, t, i * D:(i + 1) * D], ps[:, 5, i * D:(i + 1) * D],
                                                   rs[:, i:i + 1], None, ALU.mult)
                last.then_inc(S["kq_normed"], 1)

            for t in range(T):
                combine(t)
                layer_norm(x2, f_sb, [t], f"f{t}", S["fr"])
                dve.wait_ge(S["fr"], t + 1)
                nc.vector.scalar_tensor_tensor(out=xf[:, t, :], in0=f_sb[:, t, 0:D], scalar=0.5, in1=x2[:, t, :],
                                               op0=ALU.mult, op1=ALU.add)
                if t >= 1:
                    cosines(t - 1)
            cosines(T - 1)

            dve.wait_ge(S["pv2"], T)
            sums = ps[:, 4:8, D]
            nc.vector.tensor_scalar(lone[:, :], sums, 0.0, 0.5, ALU.is_equal, ALU.mult)
            then(nc.vector.tensor_scalar(den[:, 0:T], sums, LEAST_SUM, 2.0, ALU.max, ALU.mult))
            then(nc.vector.reciprocal(rec[:, 0:T], den[:, 0:T]))
            for t in range(T):
                last = nc.vector.scalar_tensor_tensor(out=x3[:, t, :], in0=ps[:, 4 + t, 0:D], scalar=rec[:, t:t + 1],
                                                      in1=xf[:, t, :], op0=ALU.mult, op1=ALU.add)
            then(last)
            for t in range(T):
                last = nc.vector.scalar_tensor_tensor(out=x3[:, t, :], in0=f_sb[:, t, 0:D], scalar=lone[:, t:t + 1],
                                                      in1=x3[:, t, :], op0=ALU.mult, op1=ALU.add)
            last.then_inc(S["x3_made"], 1)
            dve.wait_ge(S["x3_made"], 1)
            layer_norm(x3, xn, range(T), "ln4", S["ln4"])
            dve.wait_ge(S["xT4_hi"], 1)
            nc.vector.tensor_tensor(xT_lo[:, :], ps[:, 0, :], xT_hi[:, :], ALU.subtract).then_inc(S["xT4_lo"], 1)

            def split_hidden(e):
                for c in range(KT):
                    i = e * KT + c
                    dve.wait_ge(S["h_act"], i + 1)
                    if e >= 1:
                        dve.wait_ge(S["y_mm"], e)
                    nc.vector.tensor_copy(h_hi[:, c, :], hf[:, c, :]).then_inc(S["h_hi_s"], 1)
                    dve.wait_ge(S["h_hi_s"], i + 1)
                    nc.vector.tensor_tensor(h_lo[:, c, :], hf[:, c, :], h_hi[:, c, :], ALU.subtract)\
                        .then_inc(S["h_lo_s"], 1)

            def routing():
                logits_top(6, r_("bg1"), S["lg1_mm"])
                nc.vector.tensor_tensor(psum_[:, :], top[:, :, 1], top[:, :, 0], ALU.subtract)\
                    .then_inc(S["lg1_d"], 1)
                top_numbers()
                dve.wait_ge(S["lg1_tanh"], 1)
                nc.vector.tensor_scalar(w01[:, :, 0], psum_[:, :], -0.5, 0.5, ALU.mult, ALU.add)
                then(nc.vector.tensor_scalar(w01[:, :, 1], psum_[:, :], 0.5, 0.5, ALU.mult, ALU.add))
                for t in range(T):
                    last = nc.vector.tensor_scalar(oh[:, t, :], r_("iota"), topf[:, t, 1:2], w01[:, t, 1:2],
                                                   ALU.is_equal, ALU.mult)
                    nc.vector.tensor_scalar(prob[:, t, :], r_("iota"), topf[:, t, 0:1], w01[:, t, 0:1],
                                            ALU.is_equal, ALU.mult)
                then(nc.vector.tensor_copy(den[:, 0:1], rec[:, 0:1]))
                for b in (0, BLOCK):
                    last = nc.vector.tensor_tensor(gate[:, :, b:b + E], prob[:, :, :], oh[:, :, :], ALU.add)
                last.then_inc(S["gate1"], 1)
                dve.wait_ge(S["w_tr"], 1)
                then(nc.vector.tensor_copy(wT_st[0:64, :], ps[0:64, 7, :]))
                nc.vector.tensor_copy(gateT[:, :], ps[0:E, 7, :])
                b = slice(BLOCK, 2 * BLOCK)
                nc.vector.tensor_tensor(wT_st[b, :], ps[b, 7, :], wT_st[b, :], ALU.subtract).then_inc(S["w_st"], 1)

            def weigh(e):
                dve.wait_ge(S["y_mm"], e + 1)
                dve.wait_ge(S["wb_made"], e + 1)
                if e >= 3:
                    dve.wait_ge(S["acc_made"], e - 1)
                dst = acc[:, :] if e == 0 else part[:, e % 2, :]
                ins = nc.vector.tensor_tensor(dst, ps[:, 4 + e % 2, :], wb[:, e, :], ALU.mult)
                ins.then_inc(S["part_made"], 1)
                if e == 0:
                    dve.wait_ge(S["part_made"], 1)
                    nc.vector.tensor_copy(den[:, 0:1], rec[:, 0:1]).then_inc(S["acc_made"], 1)

            split_hidden(0)
            routing()
            for e in range(1, E):
                split_hidden(e)
                weigh(e - 1)
            weigh(E - 1)
            dve.wait_ge(S["fin_mm"], 1)
            for t in range(T):
                nc.vector.tensor_tensor(x3[:, t, :], x3[:, t, :], ps[:, 6, tok(t)], ALU.add)\
                    .then_inc(S["out_made"], 1)

        @block.tensor
        def _(pe):
            def mm(out_, lhsT, rhs, start=True, stop=True):
                return nc.tensor.matmul(out_, lhsT, rhs, start=start, stop=stop, skip_group_check=True)

            pe.wait_ge(S["ld_early"], 16)
            pe.wait_ge(S["msg_made"], 1)
            for h in range(H):
                if h >= 2:
                    pe.wait_ge(S["k_lo"], h - 1)
                mm(ps[:, h % 2, :], e_("wk", h, H), msgT[:, :]).then_inc(S["k_mm"], 1)
            for t in range(T):
                last = mm(ps[:, 2 + t // 2, (t % 2) * 256:(t % 2) * 256 + 256], msgT[:, tok(t)], e_("wv"))
                if t % 2:
                    last.then_inc(S["v_mm"], 1)
            pe.wait_ge(S["ln1"], T)
            for t in range(T):
                last = nc.tensor.transpose(ps[:, 4, tok(t)], xn[:, t, :], ident)
            last.then_inc(S["xT1_tr"], 1)
            pe.wait_ge(S["xT1"], 1)
            for p in range(PAIRS):
                if p < 2:
                    pe.wait_ge(S["k_lo"], H - 1 + p)
                else:
                    pe.wait_ge(S["q_lo"], p - 1)
                mm(ps[:, p % 2, :], e_("wq", p, PAIRS), xT[:, :]).then_inc(S["q_mm"], 1)
            pe.wait_ge(S["mask_made"], 1)
            pe.wait_ge(S["identb_made"], 1)
            for n in range(T):
                for t in range(T):
                    last = nc.tensor.transpose(ps[:, 4 + n, t * 64:(t + 1) * 64].bitcast(BF16), mask[:, t, tok(n)],
                                               identb[:, :])
                last.then_inc(S["mt_tr"], 1)

            def score_a(p, i):
                a, t = divmod(i, T)
                n = p * 2 * T + i
                if i == 0:
                    pe.wait_ge(S["q_lo"], PAIRS if p == 0 else p + 1)
                    pe.wait_ge(S["k_lo"], H)
                if n >= 2:
                    pe.wait_ge(S["rowmax"], n - 1)
                mm(ps[:, n % 2, :], q_st[:, p, tok(t)], k_st[:, 2 * p + a, :]).then_inc(S["sa"], 1)

            def negmax_rows(p):
                pe.wait_ge(S["negm_made"], p + 1)
                if p == 0:
                    pe.wait_ge(S["mt_made"], T)
                else:
                    pe.wait_ge(S["nm_in"], p)
                for t in range(T):
                    last = nc.tensor.transpose(ps[:, 6, tok(t)], negm[:, t, :], ident)
                last.then_inc(S["nm_tr"], 1)

            def score_b(p, i):
                a, n = divmod(i, T)
                h = 2 * p + a
                g = 2 * h + n // 2
                if i == 0:
                    pe.wait_ge(S["nm_in"], p + 1)
                if g == 0 and n == 0:
                    pe.wait_ge(S["mt_made"], T)
                    pe.wait_ge(S["v_made"], 2)
                if n % 2 == 0 and g >= 2:
                    pe.wait_ge(S["exp1"], g - 1)
                b = 2 + 2 * (g % 2) + n % 2
                mm(ps[:, b, :], identb[:, :], maskT[:, n, :], stop=False)
                last = mm(ps[:, b, :], k_st[:, h, tok(n)], q_st[:, p, :], start=False)
                if n % 2:
                    last.then_inc(S["sb_mm"], 1)

            def weighted_values(g):
                pe.wait_ge(S["exp1"], 8 * (g + 1))
                if g:
                    pe.wait_ge(S["o_normed"], g)
                for n in range(T):
                    for j in range(4):
                        last = mm(ps[BLOCK * j:BLOCK * (j + 1), 7, :],
                                  v_sb[:, n, g * P + j * BLOCK:g * P + (j + 1) * BLOCK],
                                  big[:, 4 * j + n, :], start=n == 0, stop=n == T - 1)
                last.then_inc(S["pv1"], 1)

            def outputs_back(g):
                pe.wait_ge(S["o_copied"], g + 1)
                for t in range(T):
                    last = nc.tensor.transpose(ps[:, 7, tok(t)], o_sb[:, tok(t)], ident)
                last.then_inc(S["o_tr"], 1)

            for i in range(2 * T):
                score_a(0, i)
            negmax_rows(0)
            for p in range(PAIRS):
                for i in range(2 * T):
                    if p + 1 < PAIRS:
                        score_a(p + 1, i)
                    score_b(p, i)
                if p == 1:
                    weighted_values(0)
                if p + 1 < PAIRS:
                    negmax_rows(p + 1)
                if p == 2:
                    outputs_back(0)
            weighted_values(1)
            outputs_back(1)

            pe.wait_ge(S["o_normed"], GROUPS)
            for t in range(T):
                last = nc.tensor.transpose(ps[:, 0, tok(t)], attn[:, t, :], ident)
            last.then_inc(S["at_tr"], 1)
            pe.wait_ge(S["at_copied"], 1)
            pe.wait_ge(S["ld_late"], 16)
            for t in range(T):
                last = mm(ps[:, 1, tok(t)], xT[:, tok(t)], l_("wo"))
            last.then_inc(S["op_mm"], 1)
            pe.wait_ge(S["ln2"], T)
            for t in range(T):
                last = nc.tensor.transpose(ps[:, 2, tok(t)], xn[:, t, :], ident)
            last.then_inc(S["xT2_tr"], 1)
            pe.wait_ge(S["xT2"], 1)
            for c in range(KT):
                mm(ps[:, 3 + c, :], l_("w1", c, KT), xT[:, :]).then_inc(S["h0_mm"], 1)

            def three_terms(out_, a_hi, a_lo, b_hi, b_lo, start, stop):
                mm(out_, a_hi, b_hi, start=start, stop=False)
                mm(out_, a_hi, b_lo, start=False, stop=False)
                return mm(out_, a_lo, b_hi, start=False, stop=stop)

            def experts_tile(t, after=()):
                if t >= 2:
                    pe.wait_ge(S["combined"], t - 1)
                for k in range(KT):
                    if t == 0:
                        pe.wait_ge(S["h0_lo"], k + 1)
                        pe.wait_ge(S["split"], 2 * k + 2)
                    for half in range(2):
                        c = 2 * k + half
                        last = three_terms(ps[:, 2 * (t % 2) + half, :], h_hi[:, k, tok(t)], h_lo[:, k, tok(t)],
                                           w_hi[:, c, :], w_lo[:, c, :], k == 0, k == KT - 1)
                    if k == KT - 1:
                        last.then_inc(S["gm2"], 1)
                    for at, step, tile in after:
                        if at == k:
                            step(tile)

            def features_back(t):
                pe.wait_ge(S["fr"], t + 1)
                if t:
                    pe.wait_ge(S["f_copied"], t)
                nc.tensor.transpose(ps[:, 4, 0:P], f_sb[:, t, 0:D], ident).then_inc(S["f_tr"], 1)

            def keys_queries(t):
                pe.wait_ge(S["f_copied"], t + 1)
                if t:
                    pe.wait_ge(S["kq_normed"], t)
                mm(ps[:, 5, 0:2 * D], xT[:, tok(t)], l_("wkq")).then_inc(S["kq_mm"], 1)

            def keys_queries_back(t):
                pe.wait_ge(S["kq_normed"], t + 1)
                if t:
                    pe.wait_ge(S["kq_copied"], t)
                for i in range(2):
                    last = nc.tensor.transpose(ps[:, 6, i * P:(i + 1) * P], kqn[:, t, i * D:(i + 1) * D], ident)
                last.then_inc(S["kq_tr"], 1)

            experts_tile(0)
            pe.wait_ge(S["h0_act"], KT)
            for t in range(T):
                for k in range(KT):
                    last = mm(ps[:, 7, t * E:(t + 1) * E], hf[:, k, tok(t)], l_("wg0", k, KT), k == 0, k == KT - 1)
            last.then_inc(S["lg0_mm"], 1)
            experts_tile(1)
            pe.wait_ge(S["gate0"], 1)
            for t in range(T):
                last = nc.tensor.transpose(ps[0:E, 6, tok(t)], gate[:, t, 0:E], ident)
            last.then_inc(S["g0_tr"], 1)
            pe.wait_ge(S["g0_copied"], 1)
            pe.wait_ge(S["ld_bias"], 16)
            for t in range(T):
                last = mm(ps[:, 7, tok(t)], gateT[:, tok(t)], bias_sb[:, 0:D])
            last.then_inc(S["bd_mm"], 1)
            experts_tile(2, [(1, features_back, 0), (3, keys_queries, 0)])
            experts_tile(3, [(1, keys_queries_back, 0), (2, features_back, 1), (3, keys_queries, 1)])
            keys_queries_back(1)
            for t in range(2, T):
                features_back(t)
                keys_queries(t)
                keys_queries_back(t)

            pe.wait_ge(S["combined"], T)
            pe.wait_ge(S["kq_copied"], T)
            for j in range(T):
                mm(ps[:, j, :], identb[:, :], maskT[:, j, :], stop=False)
                mm(ps[:, j, :], kqT[:, 1, tok(j)], kqT[:, 0, :], start=False).then_inc(S["at2_mm"], 1)
            pe.wait_ge(S["x2_made"], T)
            for j in range(T):
                pe.wait_ge(S["exp2"], j + 1)
                for t in range(T):
                    last = mm(ps[:, 4 + t, 0:D + 2], prob2[:, j, tok(t)], f_sb[:, j, :], j == 0, j == T - 1)
                    if j == T - 1:
                        last.then_inc(S["pv2"], 1)
            pe.wait_ge(S["ln4"], T)
            for t in range(T):
                last = nc.tensor.transpose(ps[:, 0, tok(t)], xn[:, t, :], ident)
            last.then_inc(S["xT4_tr"], 1)

            def w1_slot(e):
                return (WD_CHUNKS + 2 * e) % SLOTS

            def w2_slot(e):
                return (WD_CHUNKS + 2 * e + 1) % SLOTS

            def hidden(e):
                pe.wait_ge(S["split"], WD_CHUNKS + 2 * e + 1)
                s = w1_slot(e)
                for c in range(KT):
                    if e:
                        pe.wait_ge(S["h_act"], (e - 1) * KT + c + 1)
                    three_terms(ps[:, (c + 1) % 4, :], w_hi[:, s, tok(c)], w_lo[:, s, tok(c)], xT_hi[:, :],
                                xT_lo[:, :], True, True).then_inc(S["h_mm"], 1)

            def expert_out(e):
                pe.wait_ge(S["split"], WD_CHUNKS + 2 * e + 2)
                if e >= 2:
                    pe.wait_ge(S["part_made"], e - 1)
                s = w2_slot(e)
                for c in range(KT):
                    pe.wait_ge(S["h_lo_s"], e * KT + c + 1)
                    last = three_terms(ps[:, 4 + e % 2, :], w_hi[:, s, tok(c)], w_lo[:, s, tok(c)], h_hi[:, c, :],
                                       h_lo[:, c, :], c == 0, c == KT - 1)
                last.then_inc(S["y_mm"], 1)

            def broadcast_weights(e):
                if e >= 2:
                    pe.wait_ge(S["wb_made"], e - 1)
                mm(ps[:, 6 + e % 2, :], sel[:, e, :], wT_st[:, :]).then_inc(S["wb_mm"], 1)

            pe.wait_ge(S["xT4"], 1)
            hidden(0)
            for t in range(T):
                last = mm(ps[:, 6, t * E:(t + 1) * E], xT[:, tok(t)], l_("wg1"))
            last.then_inc(S["lg1_mm"], 1)
            pe.wait_ge(S["gate1"], 1)
            for t in range(T):
                last = nc.tensor.transpose(ps[0:64, 7, tok(t)], gate[:, t, :], ident)
            last.then_inc(S["w_tr"], 1)
            pe.wait_ge(S["w_st"], 1)
            pe.wait_ge(S["sel_made"], 1)
            broadcast_weights(0)
            for e in range(1, E):
                hidden(e)
                expert_out(e - 1)
                broadcast_weights(e)
            expert_out(E - 1)
            pe.wait_ge(S["wb_made"], E)
            for t in range(T):
                mm(ps[:, 6, tok(t)], gateT[:, tok(t)], bias_sb[:, D:2 * D], t == 0, False)
            pe.wait_ge(S["acc_made"], E - 1)
            for t in range(T):
                mm(ps[:, 6, tok(t)], acc[:, tok(t)], ident, False, False)
            pe.wait_ge(S["part_made"], E)
            for t in range(T):
                last = mm(ps[:, 6, tok(t)], part[:, (E - 1) % 2, tok(t)], ident, False, t == T - 1)
            last.then_inc(S["fin_mm"], 1)


def _layout(inputs):
    import numpy as np

    g = {k: np.asarray(v) for k, v in inputs.items()}
    f = np.float32

    wq = np.zeros((D, PAIRS, 4, BLOCK), f)
    bq = np.zeros((PAIRS, 4, BLOCK), f)
    wqT = g["L0_gnn_Wq"].T.reshape(D, PAIRS, BLOCK)
    for b in range(3):
        wq[:, :, b] = wqT
        bq[:, b] = g["L0_gnn_bq"].reshape(PAIRS, BLOCK)
    wk = np.zeros((D, H, 4, BLOCK), f)
    bk = np.zeros((H, 4, BLOCK), f)
    wkT = g["L0_gnn_Wk"].T.reshape(D, H, DH)
    for h in range(H):
        a = (h % 2) * DH
        for b in range(3):
            wk[:, h, b, a:a + DH] = wkT[:, h]
            bk[h, b, a:a + DH] = g["L0_gnn_bk"].reshape(H, DH)[h]
        bk[h, 3, h] = 1.0
    wv = np.zeros((D, H, BLOCK), f)
    bv = np.zeros((H, BLOCK), f)
    wv[:, :, 0:DH] = g["L0_gnn_Wv"].T.reshape(D, H, DH)
    bv[:, 0:DH] = g["L0_gnn_bv"].reshape(H, DH)
    bv[:, ONES_COL] = 1.0
    sel = np.zeros((P, E, P), f)
    for e in range(E):
        sel[e, e] = sel[BLOCK + e, e] = 1.0

    early = {
        "ident": np.eye(P, dtype=f),
        "e1": g["L0_gnn_E"][1][:, None],
        "bq": bq.reshape(PAIRS, P).T,
        "bk": bk.reshape(H, P).T,
        "hb1": g["L0_ffn_b1"].reshape(KT, P).T,
        "fb1": g["L1_ffn_b1"].reshape(E * KT, P).T,
        "hnT": g["L0_gnn_h_neigh"].T,
        "wk": wk.reshape(D, H * P),
        "wv": wv.reshape(D, H * BLOCK),
        "wq": wq.reshape(D, PAIRS * P),
    }
    late = {
        "wo": g["L0_gnn_Wo"].T,
        "w1": g["L0_ffn_W1"],
        "wg0": g["L0_ffn_Wg"].reshape(KT, P, E).transpose(1, 0, 2).reshape(P, KT * E),
        "wkq": np.concatenate([g["L1_gnn_Wk"].T, g["L1_gnn_Wq"].T], axis=1),
        "wg1": g["L1_ffn_Wg"],
        "sel": sel.reshape(P, E * P),
    }
    rows = {
        "bv": bv.reshape(-1), "bo": g["L0_gnn_bo"], "bg0": g["L0_ffn_bg"], "bg1": g["L1_ffn_bg"],
        "iota": np.arange(E, dtype=f),
    }
    wd = g["L0_ffn_Wd"].reshape(2, EH, KT, P, D).transpose(2, 0, 3, 1, 4).reshape(WD_CHUNKS, P, EH * D)
    w2 = g["L1_ffn_W2"].reshape(E, KT, P, D).transpose(0, 2, 1, 3).reshape(E, P, KT * D)
    w12 = np.stack([g["L1_ffn_W1"], w2], axis=1).reshape(2 * E, P, HID)
    return {
        "x": g["x"],
        "adj": g["adj"],
        "early": np.concatenate([early[k] for k in EARLY], axis=1),
        "late": np.concatenate([late[k] for k in LATE], axis=1),
        "rows": np.concatenate([rows[k] for k in ROWS]),
        "biases": np.concatenate([g["L0_ffn_bd"], g["L1_ffn_b2"]], axis=1),
        "chunks": np.concatenate([wd, w12], axis=0),
    }


def kernel(**inputs):
    import numpy as np
    import concourse.bacc as bacc
    from concourse.bass_utils import run_bass_kernel_spmd

    nc = bacc.Bacc("TRN2", target_bir_lowering=False, num_devices=1)
    arrays, args = {}, []
    for name, a in _layout(inputs).items():
        a = np.ascontiguousarray(a)
        arrays[f"in_{name}"] = a
        args.append(nc.dram_tensor(f"in_{name}", a.shape, mybir.dt.from_np(a.dtype), kind="ExternalInput").ap())
    args.append(nc.dram_tensor("out_x", (N, D), F32, kind="ExternalOutput").ap())
    build(nc, *args)
    r = run_bass_kernel_spmd(nc, [arrays], core_ids=[0])
    return r.results[0]["out_x"]
```

```python
from contextlib import ExitStack

import concourse.bass as bass
from concourse import mybir

F32 = mybir.dt.float32
F32R = mybir.dt.float32r
BF16 = mybir.dt.bfloat16
I32 = mybir.dt.int32
U32 = mybir.dt.uint32
ALU = mybir.AluOpType
ACT = mybir.ActivationFunctionType
AX = mybir.AxisListType.X

P = 128
N = 512
T = N // P
D = 128
H = 8
DH = D // H
PAIRS = H // 2
GROUPS = H // 4
HID = 512
KT = HID // P
E = 8
EH = E // 2
LN_EPS = 1e-5
COS_EPS = 1e-4
MASKED = -(2.0 ** 100)
LEAST_MAX = -(2.0 ** 60)
LEAST_SUM = 1e-30

BLOCK = 32
ONES_COL = DH
EARLY = {}
LATE = {}


def _place(table, sizes):
    at = 0
    for name, size in sizes:
        table[name] = (at, at + size)
        at += size
    return at


N_EARLY = _place(EARLY, [("e1", 1), ("bk0", 2), ("bq0", 1), ("bk", 1), ("bq", 1), ("hnT", N), ("wk0", 2 * P),
                         ("ident", P), ("wq0", P), ("wk", D), ("wq", D), ("hb1", KT), ("fb1", E * KT),
                         ("wv", 2 * P)])
N_LATE = _place(LATE, [("wo", D), ("w1", HID), ("wg0", KT * E), ("wkq", 2 * D), ("wg1", E), ("sel", E * P)])
ROWS = {}
N_ROWS = _place(ROWS, [("bv", 2 * P), ("bo", D), ("bg0", E), ("bg1", E), ("iota", E)])

N_CHUNKS = 2 * KT + 2 * E
WD_CHUNKS = 2 * KT
SLOTS = 12
STAGES = 4


POWERS = [("ln1", T), ("ln2a", 2), ("ln2b", 2), ("f0", 1), ("f1", 1), ("f2", 1), ("f3", 1), ("ln4", T)]
POWER = {}
N_POWERS = _place(POWER, POWERS)
POWER_NO = {name: i for i, (name, _) in enumerate(POWERS)}

PROJ = {"k0": 2, "k1": 3, "q0": 5, "k": 6, "q": 7}
PROJ_NO = {name: i for i, name in enumerate(PROJ)}
V_BANKS = [2, 3]
MT_BANKS = [4, 5, 7, 3]
A_LEAD = 3
STACK_DMAS = 9


WARM0 = 10


def build(nc, x, adj, early, late, rows, biases, chunks, out):
    with ExitStack() as ctx:
        def sb(name, shape, dt=F32):
            return ctx.enter_context(nc.sbuf_tensor(name, shape, dt))

        def sem(name):
            return ctx.enter_context(nc.semaphore(name))

        ps = ctx.enter_context(nc.psum_tensor("ps", [P, 8, 512], F32))

        x_sb = sb("x_sb", [P, T, D])
        early_sb = sb("early_sb", [P, N_EARLY])
        late_sb = sb("late_sb", [P, N_LATE])
        rows_sb = sb("rows_sb", [P, N_ROWS])
        bias_sb = sb("bias_sb", [E, 2 * D])
        stage = sb("stage", [P, STAGES, 512])
        adj_sb = stage[:, :, :].bitcast(I32)
        w_hi = sb("w_hi", [P, SLOTS, 512], F32R)
        w_lo = sb("w_lo", [P, SLOTS, 512], F32R)
        mask = sb("mask", [P, T, N], BF16)
        maskT = sb("maskT", [P, T, N], BF16)
        identb = sb("identb", [P, P], BF16)
        sel = sb("sel", [P, E, P], F32R)
        msgT = sb("msgT", [P, N])
        k_st = sb("k_st", [P, H, N], F32R)
        q_st = sb("q_st", [P, PAIRS, N], F32R)
        v_sb = sb("v_sb", [P, T, 2 * P])
        big = sb("big", [P, 16, 512])
        h_hi = sb("h_hi", [P, KT, 512], F32R)
        h_lo = sb("h_lo", [P, KT, 512], F32R)
        xbo = sb("xbo", [P, T, D])
        x1 = sb("x1", [P, T, D])
        x2 = sb("x2", [P, T, D])
        x3 = sb("x3", [P, T, D])
        xf = sb("xf", [P, T, D])
        f_sb = sb("f_sb", [P, T, D + 2])
        xn = sb("xn", [P, T, D])
        xT = sb("xT", [P, N])
        xT_hi = sb("xT_hi", [P, N], F32R)
        xT_lo = sb("xT_lo", [P, N], F32R)
        attn = sb("attn", [P, T, D])
        o_sb = sb("o_sb", [P, N])
        acc = o_sb
        part = sb("part", [P, 2, N])
        squares = sb("squares", [P, 2 * T, D], BF16)
        stats = sb("stats", [P, T, 6])
        mv = sb("mv", [P, T, 2])
        base = sb("base", [P, N_POWERS])
        root = sb("root", [P, N_POWERS])
        minus_half = sb("minus_half", [P, T])
        mx = sb("mx", [P, T, H])
        negm = sb("negm", [P, T, P])
        den = sb("den", [P, 2 * H])
        rec = sb("rec", [P, 2 * H])
        logit = sb("logit", [P, T, E])
        top = sb("top", [P, T, E])
        topi = sb("topi", [P, T, E], U32)
        topf = sb("topf", [P, T, E])
        prob = sb("prob", [P, T, E])
        psum_ = sb("psum_", [P, T])
        gate = sb("gate", [P, T, 64])
        gateT = sb("gateT", [E, N])
        wT_st = sb("wT_st", [P, N], F32R)
        w01 = sb("w01", [P, T, 2])
        oh = sb("oh", [P, T, E])
        ss = sb("ss", [P, T, 2])
        rs = sb("rs", [P, T, 2])
        prec = sb("prec", [P, T])
        warm = sb("warm", [P, 1])
        wg_st = sb("wg_st", [P, KT, 2 * E], F32R)
        lgT = sb("lgT", [2 * E, N])
        one_row = sb("one_row", [1, P])
        lone = sb("lone", [P, T])

        diag = xbo
        proj_hi = h_hi[:, 0:2, :]
        proj_lo = h_lo[:, 0:2, :]
        hf = big[:, 0:KT, :]
        prob2 = big[:, 0:T, :]
        kqn = big[:, 4:6, :].rearrange("p a (b c) -> p (a b) c", c=2 * D)
        kqT = big[:, 6:8, :]
        wb = big[:, 8:16, :]

        def e_(name, i=0, n=1):
            a, b = EARLY[name]
            w = (b - a) // n
            return early_sb[:, a + i * w:a + (i + 1) * w]

        def l_(name, i=0, n=1):
            a, b = LATE[name]
            w = (b - a) // n
            return late_sb[:, a + i * w:a + (i + 1) * w]

        def early_cols(first, last):
            return slice(EARLY[first][0], EARLY[last][1])

        def r_(name):
            return rows_sb[:, ROWS[name][0]:ROWS[name][1]]

        def tok(t):
            return slice(t * P, (t + 1) * P)

        ident = e_("ident")

        names = """ld_x ld_base ld_all ld_keys ld_wv ld_late ld_rows ld_bias st_out
            mask_made msg_made identb_made sel_made ln1 ln2 ln4 fr
            pr_mm pr_hi pr_lo v_mm v_made xT1_tr xT1 mt_tr mt_made
            sa rowmax negm_made nm_tr nm_in sb_mm exp1 pv1 o_copied o_tr o_normed
            at_tr at_copied op_mm x1_made xT2_tr xT2 h0_mm h0_act h0_hi h0_lo lg0_mm lg0_shift lg0_exp gate0
            g0_tr g0_copied bd_mm gm2 combined xbd_made
            lone_made diag_made f_tr f_copied kq_mm kq_ss kq_max kq_root kq_normed kq_tr kq_copied at2_mm exp2 pv2 x3_made
            xT4_tr xT4_hi xT4_lo xT4 h_mm h_act h_hi_s h_lo_s y_mm lg1_mm lg1_d lg1_tanh gate1
            w_tr w_st wb_mm wb_made part_made acc_made fin_mm out_made
            power_in power_out split wd_free w1_free w2_free chain_v chain_g pool_chain zeroed zeroed_k zeroed_w ones_made wg_hi wg_made lg0_copied lg0_tr warmed stat_made""".split()
        S = {n: sem(n) for n in names}
        ld_adj = [sem(f"ld_adj{t}") for t in range(T)]
        stacked = [sem(f"stacked{p}") for p in range(PAIRS)]
        ld_stage = [sem(f"ld_stage{i}") for i in range(STAGES)]

        block = ctx.enter_context(nc.Block())

        def half_cols(i):
            return slice(2 * i * P, 2 * (i + 1) * P)

        def chunk_free(eng, c):
            old = c - SLOTS
            if old < 0:
                return
            if old < WD_CHUNKS:
                eng.wait_ge(S["gm2"], 2 * T)
            elif (old - WD_CHUNKS) % 2 == 0:
                eng.wait_ge(S["h_mm"], KT * ((old - WD_CHUNKS) // 2 + 1))
            else:
                eng.wait_ge(S["y_mm"], (old - WD_CHUNKS) // 2 + 1)

        @block.sync
        def _(sp):
            sp.dma_start(x_sb[:, :, :], x.rearrange("(t p) d -> p t d", p=P)).then_inc(S["ld_x"], 16)
            c = early_cols("e1", "wk0")
            sp.dma_start(early_sb[:, c], early[:, c]).then_inc(S["ld_keys"], 16)
            c = early_cols("ident", "wq0")
            sp.dma_start(early_sb[:, c], early[:, c]).then_inc(S["ld_base"], 16)
            c = early_cols("wk", "fb1")
            sp.dma_start(early_sb[:, c], early[:, c]).then_inc(S["ld_all"], 16)
            adj_t = adj.rearrange("(t p) n -> t p n", p=P)
            sp.dma_start(adj_sb[:, 0, :], adj_t[0]).then_inc(ld_adj[0], 16)
            c = early_cols("wv", "wv")
            sp.dma_start(early_sb[:, c], early[:, c]).then_inc(S["ld_wv"], 16)
            for t in range(1, T):
                sp.dma_start(adj_sb[:, t, :], adj_t[t]).then_inc(ld_adj[t], 16)

            def stack(dst, src, p):
                sp.dma_start(dst.bitcast(F32), src.bitcast(F32)).then_inc(stacked[p], 16)

            for p in range(1, PAIRS):
                for part_, blocks in ((proj_hi, (0, 2)), (proj_lo, (1,))):
                    sp.wait_ge(S["pr_hi" if part_ is proj_hi else "pr_lo"], PROJ_NO["k"] + 1)
                    sp.wait_ge(S["zeroed_k"], 1)
                    for a in range(2):
                        h = 2 * p + a
                        for b in blocks:
                            to = b * BLOCK + a * DH
                            stack(k_st[to:to + DH, h, :], part_[h * DH:(h + 1) * DH, 0, :], p)
                src = slice(p * BLOCK, (p + 1) * BLOCK)
                sp.wait_ge(S["pr_hi"], PROJ_NO["q"] + 1)
                for b in range(2):
                    stack(q_st[b * BLOCK:(b + 1) * BLOCK, p, :], proj_hi[src, 1, :], p)
                sp.wait_ge(S["pr_lo"], PROJ_NO["q"] + 1)
                stack(q_st[2 * BLOCK:3 * BLOCK, p, :], proj_lo[src, 1, :], p)
            sp.dma_start(late_sb[:, :], late).then_inc(S["ld_late"], 16)
            sp.dma_start(bias_sb[:, :], biases).then_inc(S["ld_bias"], 16)
            sp.wait_ge(S["mask_made"], T)
            for c in range(N_CHUNKS):
                if c >= STAGES:
                    sp.wait_ge(S["split"], c - STAGES + 1)
                sp.dma_start(stage[:, c % STAGES, :], chunks[c]).then_inc(ld_stage[c % STAGES], 16)

        @block.gpsimd
        def _(pool):
            nc.gpsimd.memset(minus_half[:, :], -0.5)
            nc.gpsimd.memset(one_row[:, :], 1.0)
            nc.gpsimd.memset(k_st[0:3 * BLOCK, 2:H, :].bitcast(F32), 0.0).then_inc(S["zeroed_k"], 1)
            nc.gpsimd.memset(negm[:, :, :], 0.0)
            nc.gpsimd.memset(f_sb[:, :, D:D + 1], 2.0)
            nc.gpsimd.memset(f_sb[:, :, D + 1:D + 2], 0.0)
            nc.gpsimd.memset(gate[:, :, :], 0.0)
            nc.gpsimd.memset(wT_st[:, :].bitcast(F32), 0.0).then_inc(S["zeroed"], 1)

            def power(name):
                a, b = POWER[name]
                pool.wait_ge(S["power_in"], POWER_NO[name] + 1)
                nc.gpsimd.tensor_tensor(root[:, a:b], base[:, a:b], minus_half[:, 0:b - a], ALU.pow)\
                    .then_inc(S["power_out"], 1)

            def split(c):
                pool.wait_ge(ld_stage[c % STAGES], 16 * (c // STAGES + 1))
                chunk_free(pool, c)
                raw, hi, lo = stage[:, c % STAGES, :], w_hi[:, c % SLOTS, :], w_lo[:, c % SLOTS, :]
                nc.gpsimd.tensor_scalar(hi, raw, 1.0, 0.0, ALU.mult, ALU.add).then_inc(S["pool_chain"], 1)
                pool.wait_ge(S["pool_chain"], c + 1)
                nc.gpsimd.tensor_tensor(lo, raw, hi, ALU.subtract).then_inc(S["split"], 1)

            pool.wait_ge(S["zeroed"], 1)
            def norms(t):
                pool.wait_ge(S["kq_ss"], t + 1)
                nc.gpsimd.tensor_scalar(rs[:, t, :], ss[:, t, :], COS_EPS ** 2, None, ALU.max).then_inc(S["kq_max"], 1)
                pool.wait_ge(S["kq_max"], t + 1)
                nc.gpsimd.tensor_tensor(rs[:, t, :], rs[:, t, :], minus_half[:, 0:2], ALU.pow)\
                    .then_inc(S["kq_root"], 1)

            def add_part(e):
                pool.wait_ge(S["part_made"], e + 1)
                pool.wait_ge(S["acc_made"], e)
                nc.gpsimd.tensor_tensor(acc[:, :], acc[:, :], part[:, e % 2, :], ALU.add).then_inc(S["acc_made"], 1)

            power("ln1")
            for c in range(SLOTS):
                split(c)
                if c == 0:
                    pool.wait_ge(S["ld_late"], 16)
                    wg = l_("wg0").rearrange("p (k e) -> p k e", k=KT)
                    nc.gpsimd.tensor_scalar(wg_st[:, :, 0:E], wg, 1.0, 0.0, ALU.mult, ALU.add)\
                        .then_inc(S["wg_hi"], 1)
                    pool.wait_ge(S["wg_hi"], 1)
                    nc.gpsimd.tensor_tensor(wg_st[:, :, E:2 * E], wg, wg_st[:, :, 0:E], ALU.subtract)\
                        .then_inc(S["wg_made"], 1)
            power("ln2a")
            power("ln2b")
            pool.wait_ge(S["lone_made"], 1)
            for t in range(T):
                last = nc.gpsimd.tensor_tensor(diag[:, t, :], ident, lone[:, t:t + 1].to_broadcast([P, P]), ALU.mult)
            last.then_inc(S["diag_made"], 1)
            power("f0")
            power("f1")
            norms(0)
            power("f2")
            norms(1)
            power("f3")
            norms(2)
            norms(3)
            for c in range(SLOTS, SLOTS + 4):
                split(c)
            power("ln4")
            for c in range(SLOTS + 4, N_CHUNKS - 2):
                split(c)
            add_part(1)
            for c in range(N_CHUNKS - 2, N_CHUNKS):
                split(c)
            for e in range(2, E - 1):
                add_part(e)

        @block.scalar
        def _(act):
            act.dma_start(rows_sb[:, :], rows.partition_broadcast(P)).then_inc(S["ld_rows"], 16)
            act.wait_ge(S["zeroed"], 1)
            nc.scalar.activation(warm[:, :], minus_half[:, 0:1], ACT.Exp).then_inc(S["warmed"], 1)

            def key_ones(heads):
                b = slice(3 * BLOCK, 4 * BLOCK)
                col = slice(3 * BLOCK + heads.start, 3 * BLOCK + heads.stop)
                nc.scalar.copy(k_st[b, heads, :], ident[b, col].unsqueeze(2)
                               .to_broadcast([BLOCK, heads.stop - heads.start, N])).then_inc(S["ones_made"], 1)

            def project_hi(name, dst, bias):
                act.wait_ge(S["pr_mm"], PROJ_NO[name] + 1)
                nc.scalar.activation(dst, ps[:, PROJ[name], :], ACT.Identity, bias=bias).then_inc(S["pr_hi"], 1)

            act.wait_ge(S["ld_keys"], 16)
            project_hi("k0", k_st[:, 0, :], e_("bk0", 0, 2))
            project_hi("k1", k_st[:, 1, :], e_("bk0", 1, 2))
            act.wait_ge(S["xT1_tr"], 1)
            nc.scalar.copy(xT[:, :], ps[:, 4, :]).then_inc(S["xT1"], 1)
            project_hi("q0", q_st[:, 0, :], e_("bq0"))
            project_hi("k", proj_hi[:, 0, :], e_("bk"))
            project_hi("q", proj_hi[:, 1, :], e_("bq"))
            act.wait_ge(S["ld_base"], 16)
            for i in range(2):
                act.wait_ge(S["v_mm"], i + 1)
                nc.scalar.copy(v_sb[:, 2 * i:2 * i + 2, :], ps[:, V_BANKS[i], :].rearrange("p (a b) -> p a b", a=2))\
                    .then_inc(S["v_made"], 1)
            for n in range(T):
                act.wait_ge(S["mt_tr"], n + 1)
                nc.scalar.copy(maskT[:, n, :], ps[:, MT_BANKS[n], 0:256].bitcast(BF16)).then_inc(S["mt_made"], 1)
            for h in range(H):
                for half in range(2):
                    i = 2 * h + half
                    b = 2 + 2 * (i % 2)
                    act.wait_ge(S["sb_mm"], i + 1)
                    if h == 4:
                        act.wait_ge(S["pv1"], half + 1)
                    nc.scalar.activation(big[:, 4 * (h % 4) + 2 * half:4 * (h % 4) + 2 * half + 2, :],
                                         ps[:, b:b + 2, :], ACT.Exp, scale=DH ** -0.5).then_inc(S["exp1"], 1)
                if h < H // 2 - 1:
                    key_ones(slice(2 * (h + 1), 2 * (h + 2)))
                if h == 4:
                    nc.scalar.copy(o_sb[:, :], ps[:, 7, :]).then_inc(S["o_copied"], 1)
            act.wait_ge(S["warmed"], 1)
            nc.scalar.activation(warm[:, :], warm[:, :], ACT.Gelu).then_inc(S["warmed"], 1)
            act.wait_ge(S["pv1"], 4)
            act.wait_ge(S["o_tr"], 1)
            for i in range(2):
                nc.scalar.copy(o_sb[:, half_cols(i)], ps[:, 7, half_cols(i)]).then_inc(S["o_copied"], 1)
            for i in range(2):
                act.wait_ge(S["at_tr"], i + 1)
                nc.scalar.copy(xT[:, half_cols(i)], ps[:, 2 + i, 0:2 * P]).then_inc(S["at_copied"], 1)
            for i in range(2):
                act.wait_ge(S["xT2_tr"], i + 1)
                nc.scalar.copy(xT[:, half_cols(i)], ps[:, i, 0:2 * P]).then_inc(S["xT2"], 1)

            for c in range(KT):
                act.wait_ge(S["h0_mm"], c + 1)
                nc.scalar.activation(hf[:, c, :], ps[:, 3 + c, :], ACT.Gelu,
                                     bias=e_("hb1", c, KT)).then_inc(S["h0_act"], 1)
            act.wait_ge(S["lg0_mm"], 1)
            nc.scalar.copy(lgT[:, :], ps[0:2 * E, 7, :]).then_inc(S["lg0_copied"], 1)
            act.wait_ge(S["lg0_shift"], 1)
            nc.scalar.activation(prob[:, :, :], prob[:, :, :], ACT.Exp).then_inc(S["lg0_exp"], 1)

            for t in range(T):
                act.wait_ge(S["f_tr"], t + 1)
                nc.scalar.copy(xT[:, tok(t)], ps[:, 4, 0:P]).then_inc(S["f_copied"], 1)
                act.wait_ge(S["kq_mm"], t + 1)
                for i in range(2):
                    last = nc.scalar.activation(squares[:, 2 * t + i, :], ps[:, 5, i * D:(i + 1) * D], ACT.Square,
                                                accum_out=ss[:, t, i:i + 1])
                last.then_inc(S["kq_ss"], 1)
                act.wait_ge(S["kq_root"], t + 1)
                for i in range(2):
                    last = nc.scalar.activation(kqn[:, t, i * D:(i + 1) * D], ps[:, 5, i * D:(i + 1) * D], ACT.Copy,
                                                scale=rs[:, t, i:i + 1])
                last.then_inc(S["kq_normed"], 1)
                act.wait_ge(S["kq_tr"], t + 1)
                nc.scalar.copy(kqT[:, :, tok(t)], ps[:, 6, 0:2 * P].rearrange("p (a b) -> p a b", a=2))\
                    .then_inc(S["kq_copied"], 1)
            for j in range(T):
                act.wait_ge(S["at2_mm"], j + 1)
                nc.scalar.activation(prob2[:, j, :], ps[:, j, :], ACT.Exp).then_inc(S["exp2"], 1)
            act.wait_ge(S["warmed"], 2)
            nc.scalar.activation(warm[:, :], warm[:, :], ACT.Gelu).then_inc(S["warmed"], 1)
            act.wait_ge(S["xT4_tr"], 1)
            nc.scalar.copy(xT_hi[:, :], ps[:, 0, :]).then_inc(S["xT4_hi"], 1)
            act.wait_ge(S["xT4_lo"], 1)
            nc.scalar.copy(xT[:, :], ps[:, 0, :]).then_inc(S["xT4"], 1)

            def hidden(e):
                for c in range(KT):
                    i = e * KT + c
                    act.wait_ge(S["h_mm"], i + 1)
                    if i >= KT:
                        act.wait_ge(S["h_lo_s"], i - KT + 1)
                    nc.scalar.activation(hf[:, c, :], ps[:, (c + 1) % 4, :], ACT.Gelu,
                                         bias=e_("fb1", i, E * KT)).then_inc(S["h_act"], 1)

            def broadcast_copy(e):
                act.wait_ge(S["wb_mm"], e + 1)
                nc.scalar.copy(wb[:, e, :], ps[:, 6 + e % 2, :]).then_inc(S["wb_made"], 1)

            hidden(0)
            act.wait_ge(S["lg1_d"], 1)
            nc.scalar.activation(psum_[:, :], psum_[:, :], ACT.Tanh, scale=0.5).then_inc(S["lg1_tanh"], 1)
            hidden(1)
            hidden(2)
            broadcast_copy(0)
            broadcast_copy(1)
            for e in range(3, E + 1):
                if e < E:
                    hidden(e)
                broadcast_copy(e - 1)

            for t in range(T):
                act.wait_ge(S["out_made"], t + 1)
                act.dma_start(out[tok(t), :], x3[:, t, :]).then_inc(S["st_out"], 16)
            act.wait_ge(S["st_out"], 16 * T)

        @block.vector
        def _(dve):
            steps = {"n": 0, "stats": 0}

            def then(ins):
                steps["n"] += 1
                ins.then_inc(S["chain_v"], 1)
                dve.wait_ge(S["chain_v"], steps["n"])

            def power(name):
                dve.wait_ge(S["power_out"], POWER_NO[name] + 1)
                return root[:, POWER[name][0]:POWER[name][1]]

            def statistics(src, tiles):
                for t in tiles:
                    last = nc.vector.bn_stats(out=stats[:, t, :], in_=src[:, t, :])
                last.then_inc(S["stat_made"], len(tiles))
                steps["stats"] += len(tiles)

            def variances(tiles, name):
                dve.wait_ge(S["stat_made"], steps["stats"])
                for t in tiles:
                    last = nc.vector.bn_aggr(out=mv[:, t, :], in_=stats[:, t, :])
                then(last)
                a, b = POWER[name]
                nc.vector.tensor_scalar(base[:, a:b], mv[:, tiles[0]:tiles[-1] + 1, 1], LN_EPS, None, ALU.add)\
                    .then_inc(S["power_in"], 1)

            def scaled(src, dst, tiles, name, done):
                rstd = power(name)
                for i, t in enumerate(tiles):
                    nc.vector.tensor_scalar(dst[:, t, 0:D], src[:, t, :], mv[:, t, 0:1], rstd[:, i:i + 1],
                                            ALU.subtract, ALU.mult).then_inc(done, 1)

            nc.vector.memset(squares[:, 0, :], 0.0).then_inc(S["zeroed_w"], 1)
            def normalise_rows(src, dst, tiles, name, done):
                variances(tiles, name)
                scaled(src, dst, tiles, name, done)

            dve.wait_ge(S["ld_x"], 16)
            statistics(x_sb, range(T))
            variances(range(T), "ln1")

            dve.wait_ge(S["ld_keys"], 16)
            nc.vector.tensor_scalar(msgT[:, :], e_("hnT"), e_("e1"), None, ALU.add).then_inc(S["msg_made"], 1)
            scaled(x_sb, xn, range(T), "ln1", S["ln1"])

            def low_part(name, rows_, dst, high, bias):
                dve.wait_ge(S["pr_hi"], PROJ_NO[name] + 1)
                nc.vector.scalar_tensor_tensor(out=dst, in0=ps[rows_, PROJ[name], :], scalar=bias,
                                               in1=high, op0=ALU.add, op1=ALU.subtract)\
                    .then_inc(S["pr_lo"], 1)

            def make_mask(t):
                dve.wait_ge(ld_adj[t], 16)
                nc.vector.tensor_scalar(mask[:, t, :], adj_sb[:, t, :], 0.0, MASKED, ALU.is_equal, ALU.mult)\
                    .then_inc(S["mask_made"], 1)
                dve.wait_ge(S["mask_made"], t + 1)

            def row_max(p, i):
                t, a = divmod(i, 2)
                n = p * 2 * T + i
                dve.wait_ge(S["sa"], n + 1)
                nc.vector.tensor_tensor_reduce(out=ps[:, n % 2, :], in0=ps[:, n % 2, :], in1=mask[:, t, :],
                                               scale=1.0, scalar=-3e38, op0=ALU.add, op1=ALU.max,
                                               accum_out=mx[:, t, 2 * p + a:2 * p + a + 1])\
                    .then_inc(S["rowmax"], 1)

            def negate_max(p):
                dve.wait_ge(S["zeroed"], 1)
                dve.wait_ge(S["rowmax"], (p + 1) * 2 * T)
                c = 3 * BLOCK + 2 * p
                nc.vector.tensor_scalar(negm[:, :, c:c + 2], mx[:, :, 2 * p:2 * p + 2], LEAST_MAX, -1.0,
                                        ALU.max, ALU.mult).then_inc(S["negm_made"], 1)

            def max_into_queries(p):
                dve.wait_ge(S["nm_tr"], p + 1)
                b = slice(3 * BLOCK, 4 * BLOCK)
                nc.vector.tensor_copy(q_st[b, p, :], ps[b, 6, :]).then_inc(S["nm_in"], 1)

            def normalise(g, half, bank):
                dve.wait_ge(S["o_tr"], g + half + 1 if g else 1)
                o = ps[:, bank, half_cols(half)].rearrange("p (th c) -> p th c", c=BLOCK)
                r = slice(half * H, (half + 1) * H)
                then(nc.vector.tensor_scalar(den[:, r], o[:, :, ONES_COL], LEAST_SUM, None, ALU.max))
                then(nc.vector.reciprocal(rec[:, r], den[:, r]))
                last = nc.vector.tensor_tensor(
                    attn[:, 2 * half:2 * half + 2, g * 64:(g + 1) * 64].rearrange("p t (h d) -> p t h d", d=DH),
                    o[:, :, 0:DH].rearrange("p (t h) d -> p t h d", t=2),
                    rec[:, r].rearrange("p (t h) -> p t h", t=2).unsqueeze(3).to_broadcast([P, 2, 4, DH]), ALU.mult)
                last.then_inc(S["o_normed"], 1)

            second, third = slice(BLOCK, 2 * BLOCK), slice(2 * BLOCK, 3 * BLOCK)
            for a in range(2):
                low_part(f"k{a}", second, k_st[second, a, :], k_st[second, a, :], e_("bk0", a, 2)[second, :])
            low_part("q0", third, q_st[third, 0, :], q_st[third, 0, :], e_("bq0")[third, :])
            make_mask(0)
            row_max(0, 0)
            every = slice(0, P)
            low_part("k", every, proj_lo[:, 0, :], proj_hi[:, 0, :], e_("bk"))
            row_max(0, 1)
            dve.wait_ge(S["ld_base"], 16)
            nc.vector.tensor_copy(identb[:, :], ident).then_inc(S["identb_made"], 1)
            for t in range(1, T):
                make_mask(t)
                row_max(0, 2 * t)
                if t == 1:
                    low_part("q", every, proj_lo[:, 1, :], proj_hi[:, 1, :], e_("bq"))
                row_max(0, 2 * t + 1)
            for p in range(PAIRS):
                negate_max(p)
                if p + 1 < PAIRS:
                    row_max(p + 1, 0)
                    if p:
                        row_max(p + 1, 1)
                max_into_queries(p)
                if p + 1 < PAIRS:
                    for i in range(2 if p else 1, 2 * T):
                        row_max(p + 1, i)
            nc.vector.tensor_tensor(xbo[:, :, :], x_sb[:, :, :], r_("bo").unsqueeze(1).to_broadcast([P, T, D]),
                                    ALU.add)
            dve.wait_ge(S["ld_late"], 16)
            nc.vector.tensor_copy(sel[:, :, :], l_("sel").rearrange("p (e m) -> p e m", e=E))\
                .then_inc(S["sel_made"], 1)
            nc.vector.tensor_scalar(lone[:, :], mx[:, :, 0], LEAST_MAX, None, ALU.is_lt)
            for half in range(2):
                normalise(0, half, 7)
            for half in range(2):
                normalise(1, half, half)
            for i in range(2):
                dve.wait_ge(S["op_mm"], i + 1)
                nc.vector.tensor_tensor(x1[:, 2 * i:2 * i + 2, :], ps[:, 4 + i, 0:2 * P].rearrange(
                    "p (t d) -> p t d", t=2), xbo[:, 2 * i:2 * i + 2, :], ALU.add).then_inc(S["x1_made"], 1)
                dve.wait_ge(S["x1_made"], i + 1)
                statistics(x1, [2 * i, 2 * i + 1])
                variances([2 * i, 2 * i + 1], "ln2a" if i == 0 else "ln2b")
            scaled(x1, xn, [0, 1], "ln2a", S["ln2"])
            scaled(x1, xn, [2, 3], "ln2b", S["ln2"])
            nc.vector.tensor_copy(den[:, 0:1], rec[:, 0:1]).then_inc(S["lone_made"], 1)

            for c in range(KT):
                dve.wait_ge(S["h0_act"], c + 1)
                nc.vector.tensor_copy(h_hi[:, c, :], hf[:, c, :]).then_inc(S["h0_hi"], 1)
                dve.wait_ge(S["h0_hi"], c + 1)
                nc.vector.tensor_tensor(h_lo[:, c, :], hf[:, c, :], h_hi[:, c, :], ALU.subtract)\
                    .then_inc(S["h0_lo"], 1)

            def logits_top(x_, bias, x_lo=None):
                then(nc.vector.tensor_tensor(logit[:, :, :], x_, bias.unsqueeze(1).to_broadcast([P, T, E]), ALU.add))
                if x_lo is not None:
                    then(nc.vector.tensor_tensor(logit[:, :, :], logit[:, :, :], x_lo, ALU.add))
                for t in range(T):
                    last = nc.vector.max(out=top[:, t, :], in_=logit[:, t, :])
                then(last)

            def top_numbers():
                for t in range(T):
                    last = nc.vector.max_index(out=topi[:, t, :], in_max=top[:, t, :], in_values=logit[:, t, :])
                then(last)
                then(nc.vector.tensor_copy(topf[:, :, :], topi[:, :, :]))

            dve.wait_ge(S["lg0_tr"], 1)
            lg = ps[:, 6, 0:2 * T * E].rearrange("p (t e) -> p t e", t=T)
            logits_top(lg[:, :, 0:E], r_("bg0"), lg[:, :, E:2 * E])
            nc.vector.tensor_tensor(prob[:, :, :], logit[:, :, :], top[:, :, 0:1].to_broadcast([P, T, E]),
                                    ALU.subtract).then_inc(S["lg0_shift"], 1)
            top_numbers()
            dve.wait_ge(S["lg0_exp"], 1)
            then(nc.vector.tensor_reduce(psum_[:, :], prob[:, :, :], AX, ALU.add))
            then(nc.vector.reciprocal(prec[:, :], psum_[:, :]))
            for t in range(T):
                last = nc.vector.tensor_scalar(gate[:, t, 0:E], r_("iota"), topf[:, t, 0:1], prec[:, t:t + 1],
                                               ALU.is_equal, ALU.mult)
            last.then_inc(S["gate0"], 1)
            dve.wait_ge(S["gate0"], 1)
            dve.wait_ge(S["g0_tr"], 1)
            nc.vector.tensor_copy(gateT[:, :], ps[0:E, 6, :]).then_inc(S["g0_copied"], 1)

            dve.wait_ge(S["bd_mm"], 1)
            nc.vector.tensor_tensor(x1[:, :, :], x1[:, :, :], ps[:, 7, :].rearrange("p (t d) -> p t d", t=T),
                                    ALU.add).then_inc(S["xbd_made"], 1)
            dve.wait_ge(S["xbd_made"], 1)

            def combine(t):
                for half in range(2):
                    dve.wait_ge(S["gm2"], 2 * t + half + 1)
                    for e in range(half * EH, (half + 1) * EH):
                        ins = nc.vector.scalar_tensor_tensor(
                            out=x2[:, t, :], in0=ps[:, 2 * (t % 2) + half, (e % EH) * D:(e % EH + 1) * D],
                            scalar=gate[:, t, e:e + 1], in1=(x1 if e == 0 else x2)[:, t, :],
                            op0=ALU.mult, op1=ALU.add)
                        if e < E - 1:
                            then(ins)
                ins.then_inc(S["combined"], 1)
                dve.wait_ge(S["combined"], t + 1)

            for t in range(T):
                combine(t)
                statistics(x2, [t])
                normalise_rows(x2, f_sb, [t], f"f{t}", S["fr"])
            dve.wait_ge(S["fr"], T)
            then(nc.vector.scalar_tensor_tensor(out=xf[:, :, :], in0=f_sb[:, :, 0:D], scalar=0.5, in1=x2[:, :, :],
                                                op0=ALU.mult, op1=ALU.add))

            dve.wait_ge(S["pv2"], T)
            then(nc.vector.reciprocal(rec[:, 0:T], ps[:, 4:8, D]))
            for t in range(T + 1):
                if t < T:
                    nc.vector.scalar_tensor_tensor(out=x3[:, t, :], in0=ps[:, 4 + t, 0:D], scalar=rec[:, t:t + 1],
                                                   in1=xf[:, t, :], op0=ALU.mult, op1=ALU.add)\
                        .then_inc(S["x3_made"], 1)
                if t >= 1:
                    dve.wait_ge(S["x3_made"], t)
                    statistics(x3, [t - 1])
            normalise_rows(x3, xn, range(T), "ln4", S["ln4"])
            dve.wait_ge(S["xT4_hi"], 1)
            nc.vector.tensor_tensor(xT_lo[:, :], ps[:, 0, :], xT_hi[:, :], ALU.subtract).then_inc(S["xT4_lo"], 1)

            def split_hidden(e):
                for c in range(KT):
                    i = e * KT + c
                    dve.wait_ge(S["h_act"], i + 1)
                    if e >= 1:
                        dve.wait_ge(S["y_mm"], e)
                    nc.vector.tensor_copy(h_hi[:, c, :], hf[:, c, :]).then_inc(S["h_hi_s"], 1)
                    dve.wait_ge(S["h_hi_s"], i + 1)
                    nc.vector.tensor_tensor(h_lo[:, c, :], hf[:, c, :], h_hi[:, c, :], ALU.subtract)\
                        .then_inc(S["h_lo_s"], 1)

            def routing():
                dve.wait_ge(S["lg1_mm"], 1)
                logits_top(ps[:, 6, 0:T * E].rearrange("p (t e) -> p t e", t=T), r_("bg1"))
                nc.vector.tensor_tensor(psum_[:, :], top[:, :, 1], top[:, :, 0], ALU.subtract)\
                    .then_inc(S["lg1_d"], 1)
                top_numbers()
                dve.wait_ge(S["lg1_tanh"], 1)
                nc.vector.tensor_scalar(w01[:, :, 0], psum_[:, :], -0.5, 0.5, ALU.mult, ALU.add)
                then(nc.vector.tensor_scalar(w01[:, :, 1], psum_[:, :], 0.5, 0.5, ALU.mult, ALU.add))
                for t in range(T):
                    last = nc.vector.tensor_scalar(oh[:, t, :], r_("iota"), topf[:, t, 1:2], w01[:, t, 1:2],
                                                   ALU.is_equal, ALU.mult)
                    nc.vector.tensor_scalar(prob[:, t, :], r_("iota"), topf[:, t, 0:1], w01[:, t, 0:1],
                                            ALU.is_equal, ALU.mult)
                then(nc.vector.tensor_copy(den[:, 0:1], rec[:, 0:1]))
                for b in (0, BLOCK):
                    last = nc.vector.tensor_tensor(gate[:, :, b:b + E], prob[:, :, :], oh[:, :, :], ALU.add)
                last.then_inc(S["gate1"], 1)
                dve.wait_ge(S["w_tr"], 1)
                then(nc.vector.tensor_copy(wT_st[0:64, :], ps[0:64, 7, :]))
                nc.vector.tensor_copy(gateT[:, :], ps[0:E, 7, :])
                b = slice(BLOCK, 2 * BLOCK)
                nc.vector.tensor_tensor(wT_st[b, :], ps[b, 7, :], wT_st[b, :], ALU.subtract).then_inc(S["w_st"], 1)

            def weigh(e):
                dve.wait_ge(S["y_mm"], e + 1)
                dve.wait_ge(S["wb_made"], e + 1)
                if e >= 3:
                    dve.wait_ge(S["acc_made"], e - 1)
                dst = acc[:, :] if e == 0 else part[:, e % 2, :]
                ins = nc.vector.tensor_tensor(dst, ps[:, 4 + e % 2, :], wb[:, e, :], ALU.mult)
                ins.then_inc(S["part_made"], 1)
                if e == 0:
                    dve.wait_ge(S["part_made"], 1)
                    nc.vector.tensor_copy(den[:, 0:1], rec[:, 0:1]).then_inc(S["acc_made"], 1)

            split_hidden(0)
            routing()
            split_hidden(1)
            split_hidden(2)
            weigh(0)
            for e in range(3, E + 1):
                weigh(e - 2)
                if e < E:
                    split_hidden(e)
            weigh(E - 1)
            dve.wait_ge(S["fin_mm"], 1)
            for t in range(T):
                nc.vector.tensor_tensor(x3[:, t, :], x3[:, t, :], ps[:, 6, tok(t)], ALU.add)\
                    .then_inc(S["out_made"], 1)

        @block.tensor
        def _(pe):
            def mm(out_, lhsT, rhs, start=True, stop=True):
                return nc.tensor.matmul(out_, lhsT, rhs, start=start, stop=stop, skip_group_check=True)

            def keep_warm(count, bank):
                for _ in range(count):
                    mm(ps[:, bank, :], squares[:, 0, :], squares[:, 0, :].unsqueeze(1).to_broadcast([P, 4, P]))

            def project(name, w, src):
                mm(ps[:, PROJ[name], :], w, src).then_inc(S["pr_mm"], 1)

            def values(i):
                pe.wait_ge(S["ld_rows"], 16)
                pe.wait_ge(S["zeroed"], 1)
                pe.wait_ge(S["ld_wv"], 16)
                pe.wait_ge(S["pr_lo"], i + 1)
                for t in (2 * i, 2 * i + 1):
                    to = ps[:, V_BANKS[i], (t % 2) * 2 * P:(t % 2 + 1) * 2 * P]
                    mm(to, msgT[:, tok(t)], e_("wv"), stop=False)
                    last = mm(to, one_row[:, :], r_("bv")[0:1, :], start=False)
                last.then_inc(S["v_mm"], 1)

            def mask_back(n):
                pe.wait_ge(S["identb_made"], 1)
                pe.wait_ge(S["mask_made"], T)
                if MT_BANKS[n] == 4:
                    pe.wait_ge(S["xT1"], 1)
                elif MT_BANKS[n] == 3:
                    pe.wait_ge(S["v_made"], 2)
                else:
                    pe.wait_ge(S["pr_lo"], PROJ_NO["q0" if MT_BANKS[n] == 5 else "q"] + 1)
                for t in range(T):
                    last = nc.tensor.transpose(ps[:, MT_BANKS[n], t * 64:(t + 1) * 64].bitcast(BF16),
                                               mask[:, t, tok(n)], identb[:, :])
                last.then_inc(S["mt_tr"], 1)

            def score_a(p, i):
                t, a = divmod(i, 2)
                n = p * 2 * T + i
                if i == 0 and p == 0:
                    pe.wait_ge(S["pr_lo"], PROJ_NO["q0"] + 1)
                elif i == 0:
                    pe.wait_ge(stacked[p], 16 * STACK_DMAS)
                if n >= 2:
                    pe.wait_ge(S["rowmax"], n - 1)
                b = slice(0, 3 * BLOCK)
                mm(ps[:, n % 2, :], q_st[b, p, tok(t)], k_st[b, 2 * p + a, :]).then_inc(S["sa"], 1)

            def negmax_rows(p):
                pe.wait_ge(S["negm_made"], p + 1)
                if p == 0:
                    pe.wait_ge(S["pr_lo"], PROJ_NO["k"] + 1)
                else:
                    pe.wait_ge(S["nm_in"], p)
                for t in range(T):
                    last = nc.tensor.transpose(ps[:, 6, tok(t)], negm[:, t, :], ident)
                last.then_inc(S["nm_tr"], 1)

            def score_b(p, i):
                a, n = divmod(i, T)
                h = 2 * p + a
                g = 2 * h + n // 2
                if i == 0:
                    pe.wait_ge(S["nm_in"], p + 1)
                    if p:
                        pe.wait_ge(S["ones_made"], p)
                if g == 0 and n == 0:
                    pe.wait_ge(S["mt_made"], T)
                    pe.wait_ge(S["v_made"], 2)
                if n % 2 == 0 and g >= 2:
                    pe.wait_ge(S["exp1"], g - 1)
                b = 2 + 2 * (g % 2) + n % 2
                mm(ps[:, b, :], identb[:, :], maskT[:, n, :], stop=False)
                last = mm(ps[:, b, :], k_st[:, h, tok(n)], q_st[:, p, :], start=False)
                if n % 2:
                    last.then_inc(S["sb_mm"], 1)

            def weighted_values(g, half):
                pe.wait_ge(S["exp1"], 8 * g + 7 + half)
                if g and half == 0:
                    pe.wait_ge(S["o_normed"], 2)
                for n in (2 * half, 2 * half + 1):
                    for j in range(4):
                        last = mm(ps[BLOCK * j:BLOCK * (j + 1), 7, :],
                                  v_sb[:, n, g * P + j * BLOCK:g * P + (j + 1) * BLOCK],
                                  big[:, 4 * j + n, :], start=n == 0, stop=n == T - 1)
                last.then_inc(S["pv1"], 1)

            def outputs_back(g):
                pe.wait_ge(S["o_copied"], g + 1)
                for t in range(T):
                    last = nc.tensor.transpose(ps[:, 7, tok(t)], o_sb[:, tok(t)], ident)
                last.then_inc(S["o_tr"], 1)

            pe.wait_ge(S["zeroed_w"], 1)
            keep_warm(WARM0, 7)
            pe.wait_ge(S["msg_made"], 1)
            for a in range(2):
                project(f"k{a}", e_("wk0", a, 2), msgT[:, :])
            pe.wait_ge(S["ld_base"], 16)
            for t in range(T):
                pe.wait_ge(S["ln1"], t + 1)
                last = nc.tensor.transpose(ps[:, 4, tok(t)], xn[:, t, :], ident)
            last.then_inc(S["xT1_tr"], 1)
            pe.wait_ge(S["xT1"], 1)
            project("q0", e_("wq0"), xT[:, :])
            pe.wait_ge(S["ld_all"], 16)
            project("k", e_("wk"), msgT[:, :])
            project("q", e_("wq"), xT[:, :])
            woven = {1: [(values, 0)], 2: [(values, 1)],
                     7: [(mask_back, 0), (mask_back, 1), (mask_back, 2), (mask_back, 3)]}
            for n in range(2 * T + A_LEAD):
                if n == 2 * T + 1:
                    negmax_rows(0)
                score_a(n // (2 * T), n % (2 * T))
                if 3 <= n <= 6:
                    keep_warm(1, 5)
                for step, k in woven.get(n, ()):
                    step(k)
            for p in range(PAIRS):
                for i in range(2 * T):
                    n = (p + 1) * 2 * T + i + A_LEAD
                    if i == 2 * T - 1 and p + 1 < PAIRS:
                        negmax_rows(p + 1)
                    if n < PAIRS * 2 * T:
                        score_a(n // (2 * T), n % (2 * T))
                    score_b(p, i)
                    if (p, i) in ((2, 0), (2, 2)):
                        weighted_values(0, i // 2)
                    if (p, i) == (2, 6):
                        outputs_back(0)
            for half in range(2):
                weighted_values(1, half)
            keep_warm(3, 6)
            for i in range(2):
                pe.wait_ge(S["o_copied"], i + 2)
                for t in (2 * i, 2 * i + 1):
                    last = nc.tensor.transpose(ps[:, i, tok(t)], o_sb[:, tok(t)], ident)
                last.then_inc(S["o_tr"], 1)
            keep_warm(3, 6)
            pe.wait_ge(S["ld_late"], 16)
            for i in range(2):
                pe.wait_ge(S["o_normed"], i + 3)
                for t in (2 * i, 2 * i + 1):
                    last = nc.tensor.transpose(ps[:, 2 + i, (t % 2) * P:(t % 2 + 1) * P], attn[:, t, :], ident)
                last.then_inc(S["at_tr"], 1)
            for i in range(2):
                pe.wait_ge(S["at_copied"], i + 1)
                for t in (2 * i, 2 * i + 1):
                    last = mm(ps[:, 4 + i, (t % 2) * P:(t % 2 + 1) * P], xT[:, tok(t)], l_("wo"))
                last.then_inc(S["op_mm"], 1)
            keep_warm(10, 7)
            for i in range(2):
                for t in (2 * i, 2 * i + 1):
                    pe.wait_ge(S["ln2"], t + 1)
                    last = nc.tensor.transpose(ps[:, i, (t % 2) * P:(t % 2 + 1) * P], xn[:, t, :], ident)
                last.then_inc(S["xT2_tr"], 1)
            for i in range(2):
                pe.wait_ge(S["xT2"], i + 1)
                for c in range(KT):
                    last = mm(ps[:, 3 + c, half_cols(i)], l_("w1", c, KT), xT[:, half_cols(i)])
                    if i == 1:
                        last.then_inc(S["h0_mm"], 1)

            def three_terms(out_, a_hi, a_lo, b_hi, b_lo, start, stop):
                mm(out_, a_hi, b_hi, start=start, stop=False)
                mm(out_, a_hi, b_lo, start=False, stop=False)
                return mm(out_, a_lo, b_hi, start=False, stop=stop)

            def experts_tile(t, after):
                if t >= 2:
                    pe.wait_ge(S["combined"], t - 1)
                for half in range(2):
                    for k in range(KT):
                        c = 2 * k + half
                        if t == 0:
                            pe.wait_ge(S["h0_lo"], k + 1)
                            pe.wait_ge(S["split"], c + 1)
                        last = three_terms(ps[:, 2 * (t % 2) + half, :], h_hi[:, k, tok(t)], h_lo[:, k, tok(t)],
                                           w_hi[:, c, :], w_lo[:, c, :], k == 0, k == KT - 1)
                        if k == KT - 1:
                            last.then_inc(S["gm2"], 1)
                        for at, step, tile in after:
                            if at == half * KT + k:
                                step(tile)

            def features_back(t):
                pe.wait_ge(S["fr"], t + 1)
                if t:
                    pe.wait_ge(S["f_copied"], t)
                nc.tensor.transpose(ps[:, 4, 0:P], f_sb[:, t, 0:D], ident).then_inc(S["f_tr"], 1)

            def keys_queries(t):
                pe.wait_ge(S["f_copied"], t + 1)
                if t:
                    pe.wait_ge(S["kq_normed"], t)
                mm(ps[:, 5, 0:2 * D], xT[:, tok(t)], l_("wkq")).then_inc(S["kq_mm"], 1)

            def keys_queries_back(t):
                pe.wait_ge(S["kq_normed"], t + 1)
                if t:
                    pe.wait_ge(S["kq_copied"], t)
                for i in range(2):
                    last = nc.tensor.transpose(ps[:, 6, i * P:(i + 1) * P], kqn[:, t, i * D:(i + 1) * D], ident)
                last.then_inc(S["kq_tr"], 1)

            def logits(_):
                pe.wait_ge(S["wg_made"], 1)
                for k in range(KT):
                    mm(ps[0:2 * E, 7, :], wg_st[:, k, :], h_hi[:, k, :], k == 0, False)
                    last = mm(ps[0:2 * E, 7, :], wg_st[:, k, :], h_lo[:, k, :], False, k == KT - 1)
                last.then_inc(S["lg0_mm"], 1)

            def logits_back(_):
                pe.wait_ge(S["lg0_copied"], 1)
                for t in range(T):
                    last = nc.tensor.transpose(ps[:, 6, t * 2 * E:(t + 1) * 2 * E], lgT[:, tok(t)],
                                               ident[0:2 * E, 0:2 * E])
                last.then_inc(S["lg0_tr"], 1)

            def gates_back(_):
                pe.wait_ge(S["gate0"], 1)
                for t in range(T):
                    last = nc.tensor.transpose(ps[0:E, 6, tok(t)], gate[:, t, 0:E], ident)
                last.then_inc(S["g0_tr"], 1)

            def gated_bias(_):
                pe.wait_ge(S["g0_copied"], 1)
                pe.wait_ge(S["ld_bias"], 16)
                for t in range(T):
                    last = mm(ps[:, 7, tok(t)], gateT[:, tok(t)], bias_sb[:, 0:D])
                last.then_inc(S["bd_mm"], 1)

            experts_tile(0, [(3, logits, 0), (5, logits_back, 0)])
            experts_tile(1, [(1, gates_back, 0), (2, gated_bias, 0)])
            experts_tile(2, [(0, features_back, 0), (2, keys_queries, 0), (6, keys_queries_back, 0)])
            experts_tile(3, [(0, features_back, 1), (2, keys_queries, 1), (6, keys_queries_back, 1)])
            for t in range(2, T):
                features_back(t)
                keys_queries(t)
                keys_queries_back(t)

            pe.wait_ge(S["combined"], T)
            pe.wait_ge(S["kq_copied"], T)
            for j in range(T):
                mm(ps[:, j, :], identb[:, :], maskT[:, j, :], stop=False)
                mm(ps[:, j, :], kqT[:, 1, tok(j)], kqT[:, 0, :], start=False).then_inc(S["at2_mm"], 1)
            pe.wait_ge(S["diag_made"], 1)
            pe.wait_ge(S["xbd_made"], 1)
            for t in range(T):
                mm(ps[:, 4 + t, 0:D + 2], diag[:, t, :], f_sb[:, t, :], True, False)
            for j in range(T):
                pe.wait_ge(S["exp2"], j + 1)
                for t in range(T):
                    last = mm(ps[:, 4 + t, 0:D + 2], prob2[:, j, tok(t)], f_sb[:, j, :], False, j == T - 1)
                    if j == T - 1:
                        last.then_inc(S["pv2"], 1)
            for t in range(T):
                pe.wait_ge(S["ln4"], t + 1)
                last = nc.tensor.transpose(ps[:, 0, tok(t)], xn[:, t, :], ident)
            last.then_inc(S["xT4_tr"], 1)

            def w1_slot(e):
                return (WD_CHUNKS + 2 * e) % SLOTS

            def w2_slot(e):
                return (WD_CHUNKS + 2 * e + 1) % SLOTS

            def hidden(e):
                pe.wait_ge(S["split"], WD_CHUNKS + 2 * e + 1)
                s = w1_slot(e)
                for c in range(KT):
                    if e:
                        pe.wait_ge(S["h_act"], (e - 1) * KT + c + 1)
                    elif c == KT - 1:
                        pe.wait_ge(S["xT4"], 1)
                    three_terms(ps[:, (c + 1) % 4, :], w_hi[:, s, tok(c)], w_lo[:, s, tok(c)], xT_hi[:, :],
                                xT_lo[:, :], True, True).then_inc(S["h_mm"], 1)

            def expert_out(e):
                pe.wait_ge(S["split"], WD_CHUNKS + 2 * e + 2)
                if e >= 2:
                    pe.wait_ge(S["part_made"], e - 1)
                s = w2_slot(e)
                for c in range(KT):
                    pe.wait_ge(S["h_lo_s"], e * KT + c + 1)
                    last = three_terms(ps[:, 4 + e % 2, :], w_hi[:, s, tok(c)], w_lo[:, s, tok(c)], h_hi[:, c, :],
                                       h_lo[:, c, :], c == 0, c == KT - 1)
                last.then_inc(S["y_mm"], 1)

            def broadcast_weights(e):
                if e >= 2:
                    pe.wait_ge(S["wb_made"], e - 1)
                mm(ps[:, 6 + e % 2, :], sel[:, e, :], wT_st[:, :]).then_inc(S["wb_mm"], 1)

            pe.wait_ge(S["xT4_lo"], 1)
            hidden(0)
            for t in range(T):
                last = mm(ps[:, 6, t * E:(t + 1) * E], xT[:, tok(t)], l_("wg1"))
            last.then_inc(S["lg1_mm"], 1)
            hidden(1)
            expert_out(0)
            pe.wait_ge(S["gate1"], 1)
            for t in range(T):
                last = nc.tensor.transpose(ps[0:64, 7, tok(t)], gate[:, t, :], ident)
            last.then_inc(S["w_tr"], 1)
            hidden(2)
            pe.wait_ge(S["w_st"], 1)
            pe.wait_ge(S["sel_made"], 1)
            broadcast_weights(0)
            broadcast_weights(1)
            expert_out(1)
            for e in range(3, E + 1):
                if e < E:
                    hidden(e)
                broadcast_weights(e - 1)
                expert_out(e - 1)
            pe.wait_ge(S["wb_made"], E)
            for t in range(T):
                mm(ps[:, 6, tok(t)], gateT[:, tok(t)], bias_sb[:, D:2 * D], t == 0, False)
            pe.wait_ge(S["acc_made"], E - 1)
            for t in range(T):
                mm(ps[:, 6, tok(t)], acc[:, tok(t)], ident, False, False)
            pe.wait_ge(S["part_made"], E)
            for t in range(T):
                last = mm(ps[:, 6, tok(t)], part[:, (E - 1) % 2, tok(t)], ident, False, t == T - 1)
            last.then_inc(S["fin_mm"], 1)


def _layout(inputs):
    import numpy as np

    g = {k: np.asarray(v) for k, v in inputs.items()}
    f = np.float32

    wq0 = np.zeros((D, 4, BLOCK), f)
    bq0 = np.zeros((4, BLOCK), f)
    wq0[:, 0:3] = g["L0_gnn_Wq"].T[:, None, 0:BLOCK]
    bq0[0:3] = g["L0_gnn_bq"][0:BLOCK]
    wk0 = np.zeros((D, 2, 4, BLOCK), f)
    bk0 = np.zeros((2, 4, BLOCK), f)
    for h in range(2):
        a = slice(h * DH, (h + 1) * DH)
        wk0[:, h, 0:3, a] = g["L0_gnn_Wk"].T[:, None, a]
        bk0[h, 0:3, a] = g["L0_gnn_bk"][a]
        bk0[h, 3, h] = 1.0
    wv = np.zeros((D, H, BLOCK), f)
    bv = np.zeros((H, BLOCK), f)
    wv[:, :, 0:DH] = g["L0_gnn_Wv"].T.reshape(D, H, DH)
    bv[:, 0:DH] = g["L0_gnn_bv"].reshape(H, DH)
    bv[:, ONES_COL] = 1.0
    sel = np.zeros((P, E, P), f)
    for e in range(E):
        sel[e, e] = sel[BLOCK + e, e] = 1.0

    early = {
        "ident": np.eye(P, dtype=f),
        "e1": g["L0_gnn_E"][1][:, None],
        "bk0": bk0.reshape(2, P).T,
        "bq0": bq0.reshape(P, 1),
        "wk0": wk0.reshape(D, 2 * P),
        "wq0": wq0.reshape(D, P),
        "bq": g["L0_gnn_bq"][:, None],
        "bk": g["L0_gnn_bk"][:, None],
        "hb1": g["L0_ffn_b1"].reshape(KT, P).T,
        "fb1": g["L1_ffn_b1"].reshape(E * KT, P).T,
        "hnT": g["L0_gnn_h_neigh"].T,
        "wk": g["L0_gnn_Wk"].T,
        "wv": wv.reshape(D, H * BLOCK),
        "wq": g["L0_gnn_Wq"].T,
    }
    late = {
        "wo": g["L0_gnn_Wo"].T,
        "w1": g["L0_ffn_W1"],
        "wg0": g["L0_ffn_Wg"].reshape(KT, P, E).transpose(1, 0, 2).reshape(P, KT * E),
        "wkq": np.concatenate([g["L1_gnn_Wk"].T, g["L1_gnn_Wq"].T], axis=1),
        "wg1": g["L1_ffn_Wg"],
        "sel": sel.reshape(P, E * P),
    }
    rows = {
        "bv": bv.reshape(-1), "bo": g["L0_gnn_bo"], "bg0": g["L0_ffn_bg"], "bg1": g["L1_ffn_bg"],
        "iota": np.arange(E, dtype=f),
    }
    wd = g["L0_ffn_Wd"].reshape(2, EH, KT, P, D).transpose(2, 0, 3, 1, 4).reshape(WD_CHUNKS, P, EH * D)
    w2 = g["L1_ffn_W2"].reshape(E, KT, P, D).transpose(0, 2, 1, 3).reshape(E, P, KT * D)
    w12 = np.stack([g["L1_ffn_W1"], w2], axis=1).reshape(2 * E, P, HID)
    return {
        "x": g["x"],
        "adj": g["adj"],
        "early": np.concatenate([early[k] for k in EARLY], axis=1),
        "late": np.concatenate([late[k] for k in LATE], axis=1),
        "rows": np.concatenate([rows[k] for k in ROWS]),
        "biases": np.concatenate([g["L0_ffn_bd"], g["L1_ffn_b2"]], axis=1),
        "chunks": np.concatenate([wd, w12], axis=0),
    }


def kernel(**inputs):
    import numpy as np
    import concourse.bacc as bacc
    from concourse.bass_utils import run_bass_kernel_spmd

    nc = bacc.Bacc("TRN2", target_bir_lowering=False, num_devices=1)
    arrays, args = {}, []
    for name, a in _layout(inputs).items():
        a = np.ascontiguousarray(a)
        arrays[f"in_{name}"] = a
        args.append(nc.dram_tensor(f"in_{name}", a.shape, mybir.dt.from_np(a.dtype), kind="ExternalInput").ap())
    args.append(nc.dram_tensor("out_x", (N, D), F32, kind="ExternalOutput").ap())
    build(nc, *args)
    r = run_bass_kernel_spmd(nc, [arrays], core_ids=[0])
    return r.results[0]["out_x"]
```

```python
from contextlib import ExitStack

import concourse.bass as bass
from concourse import mybir

F32 = mybir.dt.float32
F32R = mybir.dt.float32r
BF16 = mybir.dt.bfloat16
I32 = mybir.dt.int32
U32 = mybir.dt.uint32
ALU = mybir.AluOpType
ACT = mybir.ActivationFunctionType
AX = mybir.AxisListType.X

P = 128
N = 512
T = N // P
D = 128
H = 8
DH = D // H
PAIRS = H // 2
GROUPS = H // 4
HID = 512
KT = HID // P
E = 8
EH = E // 2
LN_EPS = 1e-5
COS_EPS = 1e-4
MASKED = -(2.0 ** 100)
LEAST_MAX = -(2.0 ** 60)
LEAST_SUM = 1e-30

BLOCK = 32
ONES_COL = DH
EARLY = {}
LATE = {}


def _place(table, sizes):
    at = 0
    for name, size in sizes:
        table[name] = (at, at + size)
        at += size
    return at


N_EARLY = _place(EARLY, [("e1", 1), ("bk0", 2), ("bq0", 1), ("bk", 1), ("bq", 1), ("hnT", N), ("wk0", 2 * P),
                         ("ident", P), ("wq0", P), ("wk", D), ("wq", D), ("hb1", KT), ("fb1", E * KT),
                         ("wv", 2 * P)])
N_LATE = _place(LATE, [("wo", D), ("w1", HID), ("wg0", KT * E), ("wkq", 2 * D), ("wg1", E), ("sel", E * P)])
ROWS = {}
N_ROWS = _place(ROWS, [("bv", 2 * P), ("bo", D), ("bg0", E), ("bg1", E), ("iota", E)])

N_CHUNKS = 2 * KT + 2 * E
WD_CHUNKS = 2 * KT
SLOTS = 12
STAGES = 4


POWERS = [("ln1", T), ("ln2a", 2), ("ln2b", 2), ("f0", 1), ("f1", 1), ("f2", 1), ("f3", 1),
          ("ln4a", 2), ("ln4b", 2)]
POWER = {}
N_POWERS = _place(POWER, POWERS)
POWER_NO = {name: i for i, (name, _) in enumerate(POWERS)}

PROJ = {"k0": 2, "k1": 3, "q0": 5, "k": 6, "q": 7}
PROJ_NO = {name: i for i, name in enumerate(PROJ)}
V_BANKS = [2, 3]
MT_BANKS = [4, 5, 7, 3]
EXP_ORDER = [[(0, 0), (0, 1), (1, 0), (1, 1)]] * (PAIRS - 1) + [[(0, 0), (1, 0), (0, 1), (1, 1)]]
A_LEAD = 3
STACK_DMAS = 3
EARLY_SPLITS = 3


def build(nc, x, adj, early, late, rows, bd, b2, chunks, out):
    with ExitStack() as ctx:
        def sb(name, shape, dt=F32):
            return ctx.enter_context(nc.sbuf_tensor(name, shape, dt))

        def sem(name):
            return ctx.enter_context(nc.semaphore(name))

        ps = ctx.enter_context(nc.psum_tensor("ps", [P, 8, 512], F32))

        x_sb = sb("x_sb", [P, T, D])
        early_sb = sb("early_sb", [P, N_EARLY])
        late_sb = sb("late_sb", [P, N_LATE])
        rows_sb = sb("rows_sb", [P, N_ROWS])
        b2_sb = sb("b2_sb", [E, D])
        bd_st = sb("bd_st", [P, E * D], F32R)
        stage = sb("stage", [P, STAGES, 512])
        adj_sb = stage[:, :, :].bitcast(I32)
        w_hi = sb("w_hi", [P, SLOTS, 512], F32R)
        w_lo = sb("w_lo", [P, SLOTS, 512], F32R)
        mask = sb("mask", [P, T, N], BF16)
        maskT = sb("maskT", [P, T, N], BF16)
        identb = sb("identb", [P, P], BF16)
        sel = sb("sel", [P, E, P], F32R)
        msgT = sb("msgT", [P, N])
        k_st = sb("k_st", [P, H, N], F32R)
        q_st = sb("q_st", [P, PAIRS, N], F32R)
        v_sb = sb("v_sb", [P, T, 2 * P])
        big = sb("big", [P, 16, 512])
        h_hi = sb("h_hi", [P, KT, 512], F32R)
        h_lo = sb("h_lo", [P, KT, 512], F32R)
        xbo = sb("xbo", [P, T, D])
        x1 = sb("x1", [P, T, D])
        x2 = sb("x2", [P, T, D])
        x3 = sb("x3", [P, T, D])
        xf = sb("xf", [P, T, D])
        f_sb = sb("f_sb", [P, T, D + 2])
        xn = sb("xn", [P, T, D])
        xT = sb("xT", [P, N])
        xT_hi = sb("xT_hi", [P, N], F32R)
        xT_lo = sb("xT_lo", [P, N], F32R)
        attn = sb("attn", [P, T, D])
        o_sb = sb("o_sb", [P, N])
        acc = o_sb
        part = sb("part", [P, 2, N])
        bd_sb = part[0:2 * BLOCK, :, :].rearrange("p a b -> p (a b)")
        idle = sb("idle", [P, P], BF16)
        squares = sb("squares", [P, 2 * T, D], BF16)
        stats = sb("stats", [P, T, 6])
        mv = sb("mv", [P, T, 2])
        base = sb("base", [P, N_POWERS])
        root = sb("root", [P, N_POWERS])
        minus_half = sb("minus_half", [P, T])
        mx = sb("mx", [P, T, H])
        negm = sb("negm", [P, T, P])
        den = sb("den", [P, 2 * H])
        rec = sb("rec", [P, 2 * H])
        logit = sb("logit", [P, T, E])
        top = sb("top", [P, T, E])
        topi = sb("topi", [P, T, E], U32)
        topf = sb("topf", [P, T, E])
        prob = sb("prob", [P, T, E])
        psum_ = sb("psum_", [P, T])
        gate = sb("gate", [P, T, 64])
        wT_st = sb("wT_st", [P, N], F32R)
        w01 = sb("w01", [P, T, 2])
        oh = sb("oh", [P, T, E])
        ss = sb("ss", [P, T, 2])
        rs = sb("rs", [P, T, 2])
        prec = sb("prec", [P, T])
        warm = sb("warm", [P, 1])
        wg1_st = sb("wg1_st", [P, 2 * E], F32R)
        wg_st = sb("wg_st", [P, KT, 2 * E], F32R)
        lgT = sb("lgT", [2 * E, N])
        gateT = lgT[0:E, :]
        lone = sb("lone", [P, T])

        diag = xbo
        proj_hi = h_hi[:, 0:2, :]
        proj_lo = h_lo[:, 0:2, :]
        w1_hi, w1_lo = k_st[:, 0, :], k_st[:, 1, :]
        hf = big[:, 0:KT, :]
        units = [(hf, h_hi, h_lo), (big[:, KT:2 * KT, :], k_st[:, 0:KT, :], k_st[:, KT:2 * KT, :])]
        prob2 = big[:, 0:T, :]
        kqn = big[:, 4, :].rearrange("p (b c) -> p b c", c=D)
        kqT = big[:, 6:8, :]
        wb = big[:, 8:16, :]

        def e_(name, i=0, n=1):
            a, b = EARLY[name]
            w = (b - a) // n
            return early_sb[:, a + i * w:a + (i + 1) * w]

        def l_(name, i=0, n=1):
            a, b = LATE[name]
            w = (b - a) // n
            return late_sb[:, a + i * w:a + (i + 1) * w]

        def early_cols(first, last):
            return slice(EARLY[first][0], EARLY[last][1])

        def r_(name):
            return rows_sb[:, ROWS[name][0]:ROWS[name][1]]

        def tok(t):
            return slice(t * P, (t + 1) * P)

        ident = e_("ident")

        names = """ld_x ld_base ld_all ld_keys ld_wv ld_late ld_rows ld_bias st_out mask_made msg_made identb_made
            sel_made ln1 ln2 ln4 fr pr_mm pr_hi pr_lo v_mm v_made v_biased xT1_tr xT1 mt_tr mt_made sa
            rowmax negm_made nm_tr nm_in sb_mm exp1 pv1 o_copied o_tr o_normed at_tr at_copied op_mm x1_made
            xT2_tr xT2_lo xT2 h0_mm h0_act h0_hi h0_hi_a h0_lo lg0_mm lg0_shift lg0_exp gate0 gm2 combined
            xc_made lone_made diag_made f_tr f_copied kq_mm q_copied kq_ss kq_max kq_root kq_normed kq_tr
            kq_copied at2_mm exp2 pv2 x3_made xT4_tr xT4_hi xT4_lo y_half h_mm h_act h_hi_s h_hi_a
            gateT_made h_lo_s y_mm b2_mm acc_tr x4_made lg1_mm lg1_d lg1_tanh gate1 w_tr w_st wb_mm wb_made
            part_made acc_made fin_tr out_made power_in power_out split w1_high w1_made chain_v pool_chain
            zeroed zeroed_k zeroed_w ones_made wg_hi wg_made wg1_hi wg1_made bd_made ld_bd lg1_copied lg1_tr
            fs_made lg0_copied lg0_tr warmed stat_made""".split()
        S = {n: sem(n) for n in names}
        ld_adj = [sem(f"ld_adj{t}") for t in range(T)]
        stacked = [sem(f"stacked{h}") for h in range(H)]
        ld_first = [sem(f"ld_first{i}") for i in range(STAGES)]
        ld_stage = [sem(f"ld_stage{i}") for i in range(STAGES)]

        block = ctx.enter_context(nc.Block())

        old, new = slice(0, (T - 1) * P), slice((T - 1) * P, N)

        def a_step(p, i):
            return divmod(i, 2) if p == 0 else (i % T, i // T)

        def half_cols(i):
            return slice(2 * i * P, 2 * (i + 1) * P)

        def chunk_free(eng, c):
            old = c - SLOTS
            if old < 0:
                return
            if old < WD_CHUNKS:
                eng.wait_ge(S["gm2"], 2 * T)
            elif (old - WD_CHUNKS) % 2 == 0:
                eng.wait_ge(S["h_mm"], KT * ((old - WD_CHUNKS) // 2 + 1))
            else:
                eng.wait_ge(S["y_mm"], (old - WD_CHUNKS) // 2 + 1)

        @block.sync
        def _(sp):
            sp.dma_start(x_sb[:, :, :], x.rearrange("(t p) d -> p t d", p=P)).then_inc(S["ld_x"], 16)
            c = early_cols("e1", "wk0")
            sp.dma_start(early_sb[:, c], early[:, c]).then_inc(S["ld_keys"], 16)
            c = early_cols("ident", "wq0")
            sp.dma_start(early_sb[:, c], early[:, c]).then_inc(S["ld_base"], 16)
            adj_t = adj.rearrange("(t p) n -> t p n", p=P)
            sp.dma_start(adj_sb[:, 0, :], adj_t[0]).then_inc(ld_adj[0], 16)
            c = early_cols("wk", "fb1")
            sp.dma_start(early_sb[:, c], early[:, c]).then_inc(S["ld_all"], 16)
            c = early_cols("wv", "wv")
            sp.dma_start(early_sb[:, c], early[:, c]).then_inc(S["ld_wv"], 16)
            for t in range(1, T):
                sp.dma_start(adj_sb[:, t, :], adj_t[t]).then_inc(ld_adj[t], 16)

            def stack(dst, src, done):
                sp.dma_start(dst.bitcast(F32), src.bitcast(F32)).then_inc(done, 16)

            def stack_keys(p, a):
                h = 2 * p + a
                rows_ = slice(h * DH, (h + 1) * DH)
                sp.wait_ge(S["pr_hi"], PROJ_NO["k"] + 1)
                for b in (0, 2, 1):
                    if b == 1:
                        sp.wait_ge(S["pr_lo"], PROJ_NO["k"] + 1)
                    to = b * BLOCK + a * DH
                    stack(k_st[to:to + DH, h, :], (proj_lo if b == 1 else proj_hi)[rows_, 0, :], stacked[h])

            def stack_queries(p):
                rows_ = slice(p * BLOCK, (p + 1) * BLOCK)
                sp.wait_ge(S["pr_hi"], PROJ_NO["q"] + 1)
                for b in range(3):
                    if b == 2:
                        sp.wait_ge(S["pr_lo"], PROJ_NO["q"] + 1)
                    stack(q_st[b * BLOCK:(b + 1) * BLOCK, p, :], (proj_lo if b == 2 else proj_hi)[rows_, 1, :],
                          stacked[2 * p])

            sp.wait_ge(S["zeroed_k"], 1)
            for p in range(1, PAIRS):
                stack_keys(p, 0)
                stack_queries(p)
                stack_keys(p, 1)
            sp.dma_start(late_sb[:, :], late).then_inc(S["ld_late"], 16)
            sp.dma_start(bd_sb, bd.partition_broadcast(2 * BLOCK)).then_inc(S["ld_bd"], 16)
            sp.dma_start(b2_sb[:, :], b2).then_inc(S["ld_bias"], 16)
            for c in range(STAGES, N_CHUNKS):
                sp.wait_ge(S["split"], c - STAGES + 1)
                sp.dma_start(stage[:, c % STAGES, :], chunks[c]).then_inc(ld_stage[c % STAGES], 16)

        @block.gpsimd
        def _(pool):
            nc.gpsimd.memset(minus_half[:, :], -0.5)
            nc.gpsimd.memset(k_st[0:3 * BLOCK, 2:H, :].bitcast(F32), 0.0).then_inc(S["zeroed_k"], 1)
            nc.gpsimd.memset(negm[:, :, :], 0.0)
            nc.gpsimd.memset(f_sb[:, :, D:D + 1], 2.0)
            nc.gpsimd.memset(f_sb[:, :, D + 1:D + 2], 0.0)
            nc.gpsimd.memset(gate[:, :, :], 0.0)
            nc.gpsimd.memset(wT_st[:, :].bitcast(F32), 0.0).then_inc(S["zeroed"], 1)

            def power(name):
                a, b = POWER[name]
                pool.wait_ge(S["power_in"], POWER_NO[name] + 1)
                nc.gpsimd.tensor_tensor(root[:, a:b], base[:, a:b], minus_half[:, 0:b - a], ALU.pow)\
                    .then_inc(S["power_out"], 1)

            def split(c):
                if c < STAGES:
                    pool.wait_ge(ld_first[c], 16)
                else:
                    pool.wait_ge(ld_stage[c % STAGES], 16 * (c // STAGES))
                chunk_free(pool, c)
                raw, hi, lo = stage[:, c % STAGES, :], w_hi[:, c % SLOTS, :], w_lo[:, c % SLOTS, :]
                nc.gpsimd.tensor_scalar(hi, raw, 1.0, 0.0, ALU.mult, ALU.add).then_inc(S["pool_chain"], 1)
                pool.wait_ge(S["pool_chain"], c + 1)
                nc.gpsimd.tensor_tensor(lo, raw, hi, ALU.subtract).then_inc(S["split"], 1)

            def norms(t):
                pool.wait_ge(S["kq_max"], t + 1)
                nc.gpsimd.tensor_tensor(rs[:, t, :], rs[:, t, :], minus_half[:, 0:2], ALU.pow)\
                    .then_inc(S["kq_root"], 1)

            def add_part(e):
                pool.wait_ge(S["part_made"], e + 1)
                if e > 1:
                    pool.wait_ge(S["acc_made"], e - 1)
                nc.gpsimd.tensor_tensor(acc[:, :], acc[:, :], part[:, e % 2, :], ALU.add).then_inc(S["acc_made"], 1)

            pool.wait_ge(S["zeroed"], 1)
            power("ln1")
            pool.wait_ge(S["ld_base"], 16)
            nc.gpsimd.tensor_scalar(identb[:, :], ident, 1.0, 0.0, ALU.mult, ALU.add).then_inc(S["identb_made"], 1)
            for t in range(T):
                pool.wait_ge(ld_adj[t], 16)
                nc.gpsimd.tensor_scalar(mask[:, t, :], adj_sb[:, t, :], 0.0, MASKED, ALU.is_equal, ALU.mult)\
                    .then_inc(S["mask_made"], 1)
            pool.wait_ge(S["mask_made"], T)
            for c in range(STAGES):
                pool.dma_start(stage[:, c, :], chunks[c]).then_inc(ld_first[c], 16)
            for c in range(SLOTS):
                split(c)
                if c == STAGES - 1:
                    pool.wait_ge(S["v_made"], 2)
                    pool.wait_ge(S["ld_rows"], 16)
                    nc.gpsimd.tensor_tensor(v_sb[:, :, :], v_sb[:, :, :],
                                            r_("bv").unsqueeze(1).to_broadcast([P, T, 2 * P]), ALU.add)\
                        .then_inc(S["v_biased"], 1)
                if c == STAGES:
                    pool.wait_ge(S["ld_late"], 16)
                    wg = l_("wg0").rearrange("p (k e) -> p k e", k=KT)
                    nc.gpsimd.tensor_scalar(wg_st[:, :, 0:E], wg, 1.0, 0.0, ALU.mult, ALU.add)\
                        .then_inc(S["wg_hi"], 1)
                    pool.wait_ge(S["wg_hi"], 1)
                    nc.gpsimd.tensor_tensor(wg_st[:, :, E:2 * E], wg, wg_st[:, :, 0:E], ALU.subtract)\
                        .then_inc(S["wg_made"], 1)
                    nc.gpsimd.tensor_scalar(wg1_st[:, 0:E], l_("wg1"), 1.0, 0.0, ALU.mult, ALU.add)\
                        .then_inc(S["wg1_hi"], 1)
                    pool.wait_ge(S["wg1_hi"], 1)
                    nc.gpsimd.tensor_tensor(wg1_st[:, E:2 * E], l_("wg1"), wg1_st[:, 0:E], ALU.subtract)\
                        .then_inc(S["wg1_made"], 1)
            pool.wait_ge(S["sb_mm"], 2 * H)
            pool.wait_ge(S["ld_late"], 16)
            nc.gpsimd.tensor_scalar(w1_hi, l_("w1"), 1.0, 0.0, ALU.mult, ALU.add).then_inc(S["w1_high"], 1)
            pool.wait_ge(S["w1_high"], 1)
            nc.gpsimd.tensor_tensor(w1_lo, l_("w1"), w1_hi, ALU.subtract).then_inc(S["w1_made"], 1)
            power("ln2a")
            power("ln2b")
            pool.wait_ge(S["lone_made"], 1)
            pool.wait_ge(S["x1_made"], 2)
            for t in range(T):
                last = nc.gpsimd.tensor_tensor(diag[:, t, :], ident, lone[:, t:t + 1].to_broadcast([P, P]), ALU.mult)
            last.then_inc(S["diag_made"], 1)
            power("f0")
            power("f1")
            norms(0)
            power("f2")
            norms(1)
            norms(2)
            power("f3")
            norms(3)
            for c in range(SLOTS, SLOTS + EARLY_SPLITS):
                split(c)
            power("ln4a")
            power("ln4b")
            for c in range(SLOTS + EARLY_SPLITS, N_CHUNKS):
                split(c)
            for e in range(1, E - 1):
                add_part(e)

        @block.scalar
        def _(act):
            act.dma_start(rows_sb[:, :], rows.partition_broadcast(P)).then_inc(S["ld_rows"], 16)
            act.wait_ge(S["zeroed"], 1)
            nc.scalar.activation(warm[:, :], minus_half[:, 0:1], ACT.Exp).then_inc(S["warmed"], 1)

            def key_ones(heads):
                b = slice(3 * BLOCK, 4 * BLOCK)
                col = slice(3 * BLOCK + heads.start, 3 * BLOCK + heads.stop)
                nc.scalar.copy(k_st[b, heads, :], ident[b, col].unsqueeze(2)
                               .to_broadcast([BLOCK, heads.stop - heads.start, N])).then_inc(S["ones_made"], 1)

            def project_hi(name, dst, bias):
                act.wait_ge(S["pr_mm"], PROJ_NO[name] + 1)
                nc.scalar.activation(dst, ps[:, PROJ[name], :], ACT.Identity, bias=bias).then_inc(S["pr_hi"], 1)

            act.wait_ge(S["ld_keys"], 16)
            project_hi("k0", k_st[:, 0, :], e_("bk0", 0, 2))
            project_hi("k1", k_st[:, 1, :], e_("bk0", 1, 2))
            project_hi("q0", q_st[:, 0, :], e_("bq0"))
            project_hi("k", proj_hi[:, 0, :], e_("bk"))
            project_hi("q", proj_hi[:, 1, :], e_("bq"))
            act.wait_ge(S["ld_base"], 16)
            for i in range(2):
                act.wait_ge(S["v_mm"], i + 1)
                nc.scalar.copy(v_sb[:, 2 * i:2 * i + 2, :], ps[:, V_BANKS[i], :].rearrange("p (a b) -> p a b", a=2))\
                    .then_inc(S["v_made"], 1)
            for n in range(T):
                act.wait_ge(S["mt_tr"], n + 1)
                nc.scalar.copy(maskT[:, n, :], ps[:, MT_BANKS[n], 0:256].bitcast(BF16)).then_inc(S["mt_made"], 1)
            for i in range(2 * H):
                p, k = divmod(i, 4)
                a, half = EXP_ORDER[p][k]
                h = 2 * p + a
                b = 2 + 2 * (i % 2)
                act.wait_ge(S["sb_mm"], i + 1)
                if h == 4:
                    act.wait_ge(S["pv1"], half + 1)
                nc.scalar.activation(big[:, 4 * (h % 4) + 2 * half:4 * (h % 4) + 2 * half + 2, :],
                                     ps[:, b:b + 2, :], ACT.Exp, scale=DH ** -0.5).then_inc(S["exp1"], 1)
                if i % 2 and h < H // 2 - 1:
                    key_ones(slice(2 * (h + 1), 2 * (h + 2)))
                if i == 9:
                    nc.scalar.copy(o_sb[:, :], ps[:, 7, :]).then_inc(S["o_copied"], 1)
            act.wait_ge(S["warmed"], 1)
            nc.scalar.activation(warm[:, :], warm[:, :], ACT.Gelu).then_inc(S["warmed"], 1)
            act.wait_ge(S["pv1"], 4)
            act.wait_ge(S["o_tr"], 1)
            for i in range(2):
                nc.scalar.copy(o_sb[:, half_cols(i)], ps[:, 7, half_cols(i)]).then_inc(S["o_copied"], 1)
            for i in range(2):
                act.wait_ge(S["at_tr"], i + 1)
                nc.scalar.copy(xT[:, half_cols(i)], ps[:, 2 + i, 0:2 * P]).then_inc(S["at_copied"], 1)
            for i in range(2):
                act.wait_ge(S["xT2_tr"], i + 1)
                nc.scalar.copy(xT_hi[:, half_cols(i)], ps[:, i, 0:2 * P]).then_inc(S["xT2"], 1)

            for c in range(KT):
                act.wait_ge(S["h0_mm"], c + 1)
                nc.scalar.activation(hf[:, c, :], ps[:, 3 + c, :], ACT.Gelu,
                                     bias=e_("hb1", c, KT)).then_inc(S["h0_act"], 1)
                if c % 2:
                    act.wait_ge(S["h0_act"], c + 1)
                    nc.scalar.copy(h_hi[:, c, :], hf[:, c, :]).then_inc(S["h0_hi_a"], 1)
            act.wait_ge(S["lg0_mm"], 1)
            nc.scalar.copy(lgT[:, :], ps[0:2 * E, 7, :]).then_inc(S["lg0_copied"], 1)
            act.wait_ge(S["lg0_shift"], 1)
            nc.scalar.activation(prob[:, :, :], prob[:, :, :], ACT.Exp).then_inc(S["lg0_exp"], 1)

            def features_copy(t):
                act.wait_ge(S["f_tr"], t + 1)
                nc.scalar.copy(xT[:, tok(t)], ps[:, 7, 0:P]).then_inc(S["f_copied"], 1)

            def lengths(t):
                act.wait_ge(S["kq_mm"], t + 1)
                for i in range(2):
                    last = nc.scalar.activation(squares[:, 2 * t + i, :], ps[:, 5, i * D:(i + 1) * D], ACT.Square,
                                                accum_out=ss[:, t, i:i + 1])
                last.then_inc(S["kq_ss"], 1)
                nc.scalar.copy(kqT[:, 1, tok(t)], ps[:, 5, 2 * D:3 * D]).then_inc(S["q_copied"], 1)

            def keys_normed(t):
                act.wait_ge(S["kq_root"], t + 1)
                nc.scalar.activation(kqn[:, t, :], ps[:, 5, 0:D], ACT.Copy, scale=rs[:, t, 0:1])\
                    .then_inc(S["kq_normed"], 1)

            def keys_copy(t):
                act.wait_ge(S["kq_tr"], t + 1)
                nc.scalar.copy(kqT[:, 0, tok(t)], ps[:, 6, 0:P]).then_inc(S["kq_copied"], 1)

            def attend(i, j, bank, cols):
                act.wait_ge(S["at2_mm"], i + 1)
                nc.scalar.activation(prob2[:, j, cols], ps[:, bank, cols], ACT.Exp, scale=rs[:, j, 1:2])\
                    .then_inc(S["exp2"], 1)

            features_copy(0)
            lengths(0)
            keys_normed(0)
            keys_copy(0)
            features_copy(1)
            lengths(1)
            keys_normed(1)
            features_copy(2)
            keys_copy(1)
            lengths(2)
            keys_normed(2)
            keys_copy(2)
            t = T - 1
            features_copy(t)
            attend(0, 0, 2, old)
            attend(1, 1, 3, old)
            lengths(t)
            attend(2, 2, 4, old)
            keys_normed(t)
            keys_copy(t)
            attend(3, t, 7, slice(0, N))
            for j in range(t):
                attend(4 + j, j, 2 + j, new)
            act.wait_ge(S["warmed"], 2)
            nc.scalar.activation(warm[:, :], warm[:, :], ACT.Gelu).then_inc(S["warmed"], 1)
            for i in range(2):
                act.wait_ge(S["xT4_tr"], i + 1)
                nc.scalar.copy(xT_hi[:, half_cols(i)], ps[:, 4 + i, 0:2 * P]).then_inc(S["xT4_hi"], 1)

            def logits1_copy():
                act.wait_ge(S["lg1_mm"], 1)
                nc.scalar.copy(lgT[:, :], ps[0:2 * E, 6, :]).then_inc(S["lg1_copied"], 1)

            def logits1_tanh():
                act.wait_ge(S["lg1_d"], 1)
                nc.scalar.activation(psum_[:, :], psum_[:, :], ACT.Tanh, scale=0.5).then_inc(S["lg1_tanh"], 1)

            def first_broadcast_copy():
                act.wait_ge(S["w_st"], 1)
                nc.scalar.copy(gateT[:, :], ps[0:E, 6, :]).then_inc(S["gateT_made"], 1)
                broadcast_copy(0)

            def hidden(e, between={}):
                whole, high, _ = units[e % 2]
                for c in range(KT):
                    i = e * KT + c
                    act.wait_ge(S["h_mm"], i + 1)
                    if e >= 2:
                        act.wait_ge(S["h_lo_s"], i - 2 * KT + 1)
                    nc.scalar.activation(whole[:, c, :], ps[:, (c + 1) % 4, :], ACT.Gelu,
                                         bias=e_("fb1", i, E * KT)).then_inc(S["h_act"], 1)
                    if c in between:
                        between[c]()
                    if c % 2:
                        if e >= 2:
                            act.wait_ge(S["y_mm"], e - 1)
                        act.wait_ge(S["h_act"], i + 1)
                        nc.scalar.copy(high[:, c, :], whole[:, c, :]).then_inc(S["h_hi_a"], 1)

            def broadcast_copy(e):
                act.wait_ge(S["wb_mm"], e + 1)
                nc.scalar.copy(wb[:, e, :], ps[:, 6 + (e + 1) % 2, :]).then_inc(S["wb_made"], 1)

            def second_broadcast_copy():
                broadcast_copy(1)

            hidden(0, {1: logits1_copy})
            hidden(1, {1: logits1_tanh})
            hidden(2)
            for e in range(3, E):
                hidden(e, {0: first_broadcast_copy, 3: second_broadcast_copy} if e == 3 else {})
                broadcast_copy(e - 1)
            broadcast_copy(E - 1)

            for i in range(2):
                act.wait_ge(S["out_made"], i + 1)
                act.dma_start(out[half_cols(i), :].rearrange("(t p) d -> p t d", p=P), x3[:, 2 * i:2 * i + 2, :])\
                    .then_inc(S["st_out"], 16)
            act.wait_ge(S["st_out"], 16 * 2)

        @block.vector
        def _(dve):
            steps = {"n": 0, "stats": 0}

            def then(ins):
                steps["n"] += 1
                ins.then_inc(S["chain_v"], 1)
                dve.wait_ge(S["chain_v"], steps["n"])

            def power(name):
                dve.wait_ge(S["power_out"], POWER_NO[name] + 1)
                return root[:, POWER[name][0]:POWER[name][1]]

            def statistics(src, tiles):
                for t in tiles:
                    last = nc.vector.bn_stats(out=stats[:, t, :], in_=src[:, t, :])
                last.then_inc(S["stat_made"], len(tiles))
                steps["stats"] += len(tiles)

            def variances(tiles, name):
                dve.wait_ge(S["stat_made"], steps["stats"])
                for t in tiles:
                    last = nc.vector.bn_aggr(out=mv[:, t, :], in_=stats[:, t, :])
                then(last)
                a, b = POWER[name]
                nc.vector.tensor_scalar(base[:, a:b], mv[:, tiles[0]:tiles[-1] + 1, 1], LN_EPS, None, ALU.add)\
                    .then_inc(S["power_in"], 1)

            def scaled(src, dst, tiles, name, done):
                rstd = power(name)
                for i, t in enumerate(tiles):
                    nc.vector.tensor_scalar(dst[:, t, 0:D], src[:, t, :], mv[:, t, 0:1], rstd[:, i:i + 1],
                                            ALU.subtract, ALU.mult).then_inc(done, 1)

            nc.vector.memset(idle[:, :], 0.0).then_inc(S["zeroed_w"], 1)
            nc.vector.memset(bd_st[2 * BLOCK:P, :].bitcast(F32), 0.0).then_inc(S["zeroed_w"], 1)
            def normalise_rows(src, dst, tiles, name, done):
                variances(tiles, name)
                scaled(src, dst, tiles, name, done)

            dve.wait_ge(S["ld_x"], 16)
            statistics(x_sb, range(T))
            variances(range(T), "ln1")

            dve.wait_ge(S["ld_keys"], 16)
            nc.vector.tensor_scalar(msgT[:, :], e_("hnT"), e_("e1"), None, ALU.add).then_inc(S["msg_made"], 1)
            scaled(x_sb, xn, range(T), "ln1", S["ln1"])

            def low_part(name, rows_, dst, high, bias):
                dve.wait_ge(S["pr_hi"], PROJ_NO[name] + 1)
                nc.vector.scalar_tensor_tensor(out=dst, in0=ps[rows_, PROJ[name], :], scalar=bias,
                                               in1=high, op0=ALU.add, op1=ALU.subtract)\
                    .then_inc(S["pr_lo"], 1)

            def row_max(p, i):
                t, a = a_step(p, i)
                n = p * 2 * T + i
                dve.wait_ge(S["sa"], n + 1)
                if p == 0 and a == 0:
                    dve.wait_ge(S["mask_made"], t + 1)
                nc.vector.tensor_tensor_reduce(out=ps[:, n % 2, :], in0=ps[:, n % 2, :], in1=mask[:, t, :],
                                               scale=1.0, scalar=-3e38, op0=ALU.add, op1=ALU.max,
                                               accum_out=mx[:, t, 2 * p + a:2 * p + a + 1])\
                    .then_inc(S["rowmax"], 1)

            def negate_max(p):
                dve.wait_ge(S["zeroed"], 1)
                dve.wait_ge(S["rowmax"], (p + 1) * 2 * T)
                c = 3 * BLOCK + 2 * p
                nc.vector.tensor_scalar(negm[:, :, c:c + 2], mx[:, :, 2 * p:2 * p + 2], LEAST_MAX, -1.0,
                                        ALU.max, ALU.mult).then_inc(S["negm_made"], 1)

            def max_into_queries(p):
                dve.wait_ge(S["nm_tr"], p + 1)
                b = slice(3 * BLOCK, 4 * BLOCK)
                nc.vector.tensor_copy(q_st[b, p, :], ps[b, 6, :]).then_inc(S["nm_in"], 1)

            def normalise(g, half, bank):
                dve.wait_ge(S["o_tr"], g + half + 1 if g else 1)
                o = ps[:, bank, half_cols(half)].rearrange("p (th c) -> p th c", c=BLOCK)
                r = slice(half * H, (half + 1) * H)
                then(nc.vector.tensor_scalar(den[:, r], o[:, :, ONES_COL], LEAST_SUM, None, ALU.max))
                then(nc.vector.reciprocal(rec[:, r], den[:, r]))
                last = nc.vector.tensor_tensor(
                    attn[:, 2 * half:2 * half + 2, g * 64:(g + 1) * 64].rearrange("p t (h d) -> p t h d", d=DH),
                    o[:, :, 0:DH].rearrange("p (t h) d -> p t h d", t=2),
                    rec[:, r].rearrange("p (t h) -> p t h", t=2).unsqueeze(3).to_broadcast([P, 2, 4, DH]), ALU.mult)
                last.then_inc(S["o_normed"], 1)

            dve.wait_ge(S["xT1_tr"], 1)
            nc.vector.tensor_copy(xT[:, :], ps[:, 4, :]).then_inc(S["xT1"], 1)

            second, third = slice(BLOCK, 2 * BLOCK), slice(2 * BLOCK, 3 * BLOCK)
            for a in range(2):
                low_part(f"k{a}", second, k_st[second, a, :], k_st[second, a, :], e_("bk0", a, 2)[second, :])
            low_part("q0", third, q_st[third, 0, :], q_st[third, 0, :], e_("bq0")[third, :])
            row_max(0, 0)
            every = slice(0, P)
            low_part("k", every, proj_lo[:, 0, :], proj_hi[:, 0, :], e_("bk"))
            low_part("q", every, proj_lo[:, 1, :], proj_hi[:, 1, :], e_("bq"))
            row_max(0, 1)
            for t in range(1, T):
                row_max(0, 2 * t)
                row_max(0, 2 * t + 1)
            for p in range(PAIRS):
                negate_max(p)
                if p + 1 < PAIRS:
                    row_max(p + 1, 0)
                    if p:
                        row_max(p + 1, 1)
                max_into_queries(p)
                if p + 1 < PAIRS:
                    for i in range(2 if p else 1, 2 * T):
                        row_max(p + 1, i)
            for half in range(2):
                normalise(0, half, 7)
            nc.vector.tensor_tensor(xbo[:, :, :], x_sb[:, :, :], r_("bo").unsqueeze(1).to_broadcast([P, T, D]),
                                    ALU.add)
            dve.wait_ge(S["ld_late"], 16)
            nc.vector.tensor_copy(sel[:, :, :], l_("sel").rearrange("p (e m) -> p e m", e=E))\
                .then_inc(S["sel_made"], 1)
            both, low = slice(0, 2 * BLOCK), slice(BLOCK, 2 * BLOCK)
            dve.wait_ge(S["ld_bd"], 16)
            then(nc.vector.tensor_copy(bd_st[both, :], bd_sb))
            nc.vector.tensor_tensor(bd_st[low, :], bd_sb[low, :], bd_st[low, :], ALU.subtract)\
                .then_inc(S["bd_made"], 1)
            nc.vector.tensor_scalar(lone[:, :], mx[:, :, 0], LEAST_MAX, None, ALU.is_lt).then_inc(S["lone_made"], 1)
            for half in range(2):
                normalise(1, half, half)
            for i in range(2):
                dve.wait_ge(S["op_mm"], i + 1)
                nc.vector.tensor_tensor(x1[:, 2 * i:2 * i + 2, :], ps[:, 4 + i, 0:2 * P].rearrange(
                    "p (t d) -> p t d", t=2), xbo[:, 2 * i:2 * i + 2, :], ALU.add).then_inc(S["x1_made"], 1)
                dve.wait_ge(S["x1_made"], i + 1)
                statistics(x1, [2 * i, 2 * i + 1])
                variances([2 * i, 2 * i + 1], "ln2a" if i == 0 else "ln2b")
            scaled(x1, xn, [0, 1], "ln2a", S["ln2"])
            scaled(x1, xn, [2, 3], "ln2b", S["ln2"])

            for i in range(2):
                dve.wait_ge(S["xT2"], i + 1)
                nc.vector.tensor_tensor(xT_lo[:, half_cols(i)], ps[:, i, 0:2 * P], xT_hi[:, half_cols(i)],
                                        ALU.subtract).then_inc(S["xT2_lo"], 1)

            for c in range(KT):
                if c % 2 == 0:
                    dve.wait_ge(S["h0_act"], c + 1)
                    nc.vector.tensor_copy(h_hi[:, c, :], hf[:, c, :]).then_inc(S["h0_hi"], 1)
                dve.wait_ge(S["h0_hi_a" if c % 2 else "h0_hi"], c // 2 + 1)
                nc.vector.tensor_tensor(h_lo[:, c, :], hf[:, c, :], h_hi[:, c, :], ALU.subtract)\
                    .then_inc(S["h0_lo"], 1)

            def logits_top(x_, bias, x_lo=None):
                then(nc.vector.tensor_tensor(logit[:, :, :], x_, bias.unsqueeze(1).to_broadcast([P, T, E]), ALU.add))
                if x_lo is not None:
                    then(nc.vector.tensor_tensor(logit[:, :, :], logit[:, :, :], x_lo, ALU.add))
                for t in range(T):
                    last = nc.vector.max(out=top[:, t, :], in_=logit[:, t, :])
                then(last)

            def top_numbers():
                for t in range(T):
                    last = nc.vector.max_index(out=topi[:, t, :], in_max=top[:, t, :], in_values=logit[:, t, :])
                then(last)
                then(nc.vector.tensor_copy(topf[:, :, :], topi[:, :, :]))

            def one_hot(dst, k):
                return nc.vector.tensor_tensor(dst[:, :, :], r_("iota").unsqueeze(1).to_broadcast([P, T, E]),
                                               topf[:, :, k:k + 1].to_broadcast([P, T, E]), ALU.is_equal)

            dve.wait_ge(S["lg0_tr"], 1)
            lg = ps[:, 6, 0:2 * T * E].rearrange("p (t e) -> p t e", t=T)
            logits_top(lg[:, :, 0:E], r_("bg0"), lg[:, :, E:2 * E])
            nc.vector.tensor_tensor(prob[:, :, :], logit[:, :, :], top[:, :, 0:1].to_broadcast([P, T, E]),
                                    ALU.subtract).then_inc(S["lg0_shift"], 1)
            top_numbers()
            dve.wait_ge(S["lg0_exp"], 1)
            then(nc.vector.tensor_reduce(psum_[:, :], prob[:, :, :], AX, ALU.add))
            one_hot(oh, 0)
            then(nc.vector.reciprocal(prec[:, :], psum_[:, :]))
            last = nc.vector.tensor_tensor(gate[:, :, 0:E], oh[:, :, :], prec[:, :].unsqueeze(2)
                                           .to_broadcast([P, T, E]), ALU.mult)
            last.then_inc(S["gate0"], 1)
            dve.wait_ge(S["gate0"], 1)

            def combine(t, half):
                dve.wait_ge(S["gm2"], 2 * t + half + 1)
                for e in range(half * EH, (half + 1) * EH):
                    ins = nc.vector.scalar_tensor_tensor(
                        out=x2[:, t, :], in0=ps[:, 2 * ((t + 1) % 2) + half, (e % EH) * D:(e % EH + 1) * D],
                        scalar=gate[:, t, e:e + 1], in1=(x1 if e == 0 else x2)[:, t, :],
                        op0=ALU.mult, op1=ALU.add)
                    if e % EH < EH - 1:
                        then(ins)
                ins.then_inc(S["combined"], 1)
                dve.wait_ge(S["combined"], 2 * t + half + 1)

            def bound(t):
                dve.wait_ge(S["kq_ss"], t + 1)
                a = POWER[f"f{t}"][0]
                nc.vector.scalar_tensor_tensor(out=rs[:, t, :], in0=base[:, a:a + 1].to_broadcast([P, 2]),
                                               scalar=COS_EPS ** 2, in1=ss[:, t, :], op0=ALU.mult, op1=ALU.max)\
                    .then_inc(S["kq_max"], 1)

            for t in range(T):
                combine(t, 0)
                if t:
                    scaled(x2, f_sb, [t - 1], f"f{t - 1}", S["fr"])
                if t == T - 1:
                    bound(t - 1)
                combine(t, 1)
                statistics(x2, [t])
                variances([t], f"f{t}")
                nc.vector.tensor_scalar(xn[:, t, :], x2[:, t, :], mv[:, t, 0:1], None, ALU.subtract)\
                    .then_inc(S["xc_made"], 1)
                if 0 < t < T - 1:
                    bound(t - 1)
            scaled(x2, f_sb, [T - 1], f"f{T - 1}", S["fr"])
            bound(T - 1)
            dve.wait_ge(S["fr"], T)
            nc.vector.scalar_tensor_tensor(out=xf[:, :, :], in0=f_sb[:, :, 0:D], scalar=0.5, in1=x2[:, :, :],
                                           op0=ALU.mult, op1=ALU.add).then_inc(S["fs_made"], 1)

            dve.wait_ge(S["fs_made"], 1)
            for i in range(2):
                dve.wait_ge(S["pv2"], i + 1)
                a = ps[:, i, 0:2 * (D + 2)].rearrange("p (t d) -> p t d", t=2)
                tiles = [2 * i, 2 * i + 1]
                then(nc.vector.reciprocal(rec[:, 2 * i:2 * i + 2], a[:, :, D]))
                for k, t in enumerate(tiles):
                    nc.vector.scalar_tensor_tensor(out=x3[:, t, :], in0=a[:, k, 0:D], scalar=rec[:, t:t + 1],
                                                   in1=xf[:, t, :], op0=ALU.mult, op1=ALU.add)\
                        .then_inc(S["x3_made"], 1)
                for t in tiles:
                    dve.wait_ge(S["x3_made"], t + 1)
                    statistics(x3, [t])
                variances(tiles, "ln4a" if i == 0 else "ln4b")
            scaled(x3, xn, [0, 1], "ln4a", S["ln4"])
            scaled(x3, xn, [2, 3], "ln4b", S["ln4"])
            for i in range(2):
                dve.wait_ge(S["xT4_hi"], i + 1)
                nc.vector.tensor_tensor(xT_lo[:, half_cols(i)], ps[:, 4 + i, 0:2 * P], xT_hi[:, half_cols(i)],
                                        ALU.subtract).then_inc(S["xT4_lo"], 1)

            def split_hidden(e, tiles=range(KT)):
                whole, high, low = units[e % 2]
                for c in tiles:
                    i = e * KT + c
                    if e >= 2:
                        dve.wait_ge(S["y_mm"], e - 1)
                    if c % 2 == 0:
                        dve.wait_ge(S["h_act"], i + 1)
                        nc.vector.tensor_copy(high[:, c, :], whole[:, c, :]).then_inc(S["h_hi_s"], 1)
                    dve.wait_ge(S["h_hi_a" if c % 2 else "h_hi_s"], i // 2 + 1)
                    nc.vector.tensor_tensor(low[:, c, :], whole[:, c, :], high[:, c, :], ALU.subtract)\
                        .then_inc(S["h_lo_s"], 1)

            def routing():
                dve.wait_ge(S["lg1_tr"], 1)
                lg = ps[:, 7, 0:2 * T * E].rearrange("p (t e) -> p t e", t=T)
                logits_top(lg[:, :, 0:E], r_("bg1"), lg[:, :, E:2 * E])
                nc.vector.tensor_tensor(psum_[:, :], top[:, :, 1], top[:, :, 0], ALU.subtract)\
                    .then_inc(S["lg1_d"], 1)
                top_numbers()
                dve.wait_ge(S["lg1_tanh"], 1)
                nc.vector.tensor_scalar(w01[:, :, 0], psum_[:, :], -0.5, 0.5, ALU.mult, ALU.add)
                then(nc.vector.tensor_scalar(w01[:, :, 1], psum_[:, :], 0.5, 0.5, ALU.mult, ALU.add))
                one_hot(oh, 1)
                then(one_hot(prob, 0))
                nc.vector.tensor_tensor(oh[:, :, :], oh[:, :, :], w01[:, :, 1:2].to_broadcast([P, T, E]), ALU.mult)
                then(nc.vector.tensor_tensor(prob[:, :, :], prob[:, :, :], w01[:, :, 0:1].to_broadcast([P, T, E]),
                                             ALU.mult))
                for b in (0, BLOCK):
                    last = nc.vector.tensor_tensor(gate[:, :, b:b + E], prob[:, :, :], oh[:, :, :], ALU.add)
                last.then_inc(S["gate1"], 1)

            def weights_split():
                dve.wait_ge(S["w_tr"], 1)
                then(nc.vector.tensor_copy(wT_st[0:64, :], ps[0:64, 6, :]))
                b = slice(BLOCK, 2 * BLOCK)
                nc.vector.tensor_tensor(wT_st[b, :], ps[b, 6, :], wT_st[b, :], ALU.subtract).then_inc(S["w_st"], 1)

            def weigh(e):
                dve.wait_ge(S["y_mm"], e + 1)
                dve.wait_ge(S["wb_made"], e + 1)
                if e >= 3:
                    dve.wait_ge(S["acc_made"], e - 2)
                dst = acc[:, :] if e == 0 else part[:, e % 2, :]
                ins = nc.vector.tensor_tensor(dst, ps[:, 4 + e % 2, :], wb[:, e, :], ALU.mult)
                ins.then_inc(S["part_made"], 1)

            split_hidden(0)
            routing()
            split_hidden(1)
            weights_split()
            for e in range(2, E):
                split_hidden(e, [0, 1])
                weigh(e - 2)
                split_hidden(e, [2, 3])
            weigh(E - 2)
            dve.wait_ge(S["b2_mm"], 1)
            all4 = "p (t d) -> p t d"
            nc.vector.tensor_tensor(x3[:, :, :], x3[:, :, :], ps[:, 0, :].rearrange(all4, t=T), ALU.add)\
                .then_inc(S["x4_made"], 1)

            def weigh_last(i):
                dve.wait_ge(S["y_half"], i + 1)
                dve.wait_ge(S["wb_made"], E)
                dve.wait_ge(S["acc_made"], E - 3)
                nc.vector.tensor_tensor(part[:, (E - 1) % 2, half_cols(i)], ps[:, 5 - i, half_cols(i)],
                                        wb[:, E - 1, half_cols(i)], ALU.mult).then_inc(S["part_made"], 1)

            weigh_last(0)
            dve.wait_ge(S["acc_tr"], 1)
            dve.wait_ge(S["x4_made"], 1)
            nc.vector.tensor_tensor(x3[:, :, :], x3[:, :, :], ps[:, 1, :].rearrange(all4, t=T), ALU.add)\
                .then_inc(S["x4_made"], 1)
            weigh_last(1)
            dve.wait_ge(S["x4_made"], 2)
            for i in range(2):
                dve.wait_ge(S["fin_tr"], i + 1)
                tiles = slice(2 * i, 2 * i + 2)
                nc.vector.tensor_tensor(x3[:, tiles, :], x3[:, tiles, :], ps[:, 2 + i, 0:2 * P].rearrange(
                    all4, t=2), ALU.add).then_inc(S["out_made"], 1)

        @block.tensor
        def _(pe):
            def mm(out_, lhsT, rhs, start=True, stop=True):
                return nc.tensor.matmul(out_, lhsT, rhs, start=start, stop=stop, skip_group_check=True)

            def keep_warm(count, bank):
                for _ in range(count):
                    mm(ps[:, bank, :], idle[:, :], idle[:, :].unsqueeze(1).to_broadcast([P, 4, P]))

            def project(name, w, src):
                mm(ps[:, PROJ[name], :], w, src).then_inc(S["pr_mm"], 1)

            def values(i):
                pe.wait_ge(S["ld_wv"], 16)
                pe.wait_ge(S["pr_lo"], i + 1)
                for t in (2 * i, 2 * i + 1):
                    to = ps[:, V_BANKS[i], (t % 2) * 2 * P:(t % 2 + 1) * 2 * P]
                    last = mm(to, msgT[:, tok(t)], e_("wv"))
                last.then_inc(S["v_mm"], 1)

            def mask_back(n):
                pe.wait_ge(S["identb_made"], 1)
                pe.wait_ge(S["mask_made"], T)
                if MT_BANKS[n] == 4:
                    pe.wait_ge(S["xT1"], 1)
                elif MT_BANKS[n] == 3:
                    pe.wait_ge(S["v_made"], 2)
                else:
                    pe.wait_ge(S["pr_lo"], PROJ_NO["q0" if MT_BANKS[n] == 5 else "q"] + 1)
                for t in range(T):
                    last = nc.tensor.transpose(ps[:, MT_BANKS[n], t * 64:(t + 1) * 64].bitcast(BF16),
                                               mask[:, t, tok(n)], identb[:, :])
                last.then_inc(S["mt_tr"], 1)

            def score_a(p, i):
                t, a = a_step(p, i)
                n = p * 2 * T + i
                if i == 0 and p == 0:
                    pe.wait_ge(S["pr_lo"], PROJ_NO["q0"] + 1)
                elif i % T == 0 and p:
                    pe.wait_ge(stacked[2 * p + a], 16 * (STACK_DMAS if a else 2 * STACK_DMAS))
                if n >= 2:
                    pe.wait_ge(S["rowmax"], n - 1)
                b = slice(0, 3 * BLOCK)
                mm(ps[:, n % 2, :], q_st[b, p, tok(t)], k_st[b, 2 * p + a, :]).then_inc(S["sa"], 1)

            def negmax_rows(p):
                pe.wait_ge(S["negm_made"], p + 1)
                if p == 0:
                    pe.wait_ge(S["pr_lo"], PROJ_NO["k"] + 1)
                else:
                    pe.wait_ge(S["nm_in"], p)
                for t in range(T):
                    last = nc.tensor.transpose(ps[:, 6, tok(t)], negm[:, t, :], ident)
                last.then_inc(S["nm_tr"], 1)

            def score_b(p, i):
                a, half = EXP_ORDER[p][i // 2]
                n = 2 * half + i % 2
                h = 2 * p + a
                g = 4 * p + i // 2
                if i == 0:
                    pe.wait_ge(S["nm_in"], p + 1)
                    if p:
                        pe.wait_ge(S["ones_made"], p)
                if g == 0 and n == 0:
                    pe.wait_ge(S["mt_made"], T)
                    pe.wait_ge(S["v_made"], 2)
                if n % 2 == 0 and g >= 2:
                    pe.wait_ge(S["exp1"], g - 1)
                b = 2 + 2 * (g % 2) + n % 2
                mm(ps[:, b, :], identb[:, :], maskT[:, n, :], stop=False)
                last = mm(ps[:, b, :], k_st[:, h, tok(n)], q_st[:, p, :], start=False)
                if n % 2:
                    last.then_inc(S["sb_mm"], 1)

            def weighted_values(g, half):
                pe.wait_ge(S["exp1"], 8 + 6 * g + 2 * half if g else 7 + half)
                pe.wait_ge(S["v_biased"], 1)
                if g and half == 0:
                    pe.wait_ge(S["o_normed"], 2)
                for n in (2 * half, 2 * half + 1):
                    for j in range(4):
                        last = mm(ps[BLOCK * j:BLOCK * (j + 1), 7, :],
                                  v_sb[:, n, g * P + j * BLOCK:g * P + (j + 1) * BLOCK],
                                  big[:, 4 * j + n, :], start=n == 0, stop=n == T - 1)
                last.then_inc(S["pv1"], 1)

            def outputs_back(g):
                pe.wait_ge(S["o_copied"], g + 1)
                for t in range(T):
                    last = nc.tensor.transpose(ps[:, 7, tok(t)], o_sb[:, tok(t)], ident)
                last.then_inc(S["o_tr"], 1)

            pe.wait_ge(S["zeroed_w"], 1)
            keep_warm(10, 7)
            pe.wait_ge(S["msg_made"], 1)
            project("k0", e_("wk0", 0, 2), msgT[:, :])
            pe.wait_ge(S["ld_base"], 16)
            for t in range(T):
                pe.wait_ge(S["ln1"], t + 1)
                last = nc.tensor.transpose(ps[:, 4, tok(t)], xn[:, t, :], ident)
            last.then_inc(S["xT1_tr"], 1)
            project("k1", e_("wk0", 1, 2), msgT[:, :])
            pe.wait_ge(S["xT1"], 1)
            project("q0", e_("wq0"), xT[:, :])
            pe.wait_ge(S["ld_all"], 16)
            project("k", e_("wk"), msgT[:, :])
            project("q", e_("wq"), xT[:, :])
            woven = {1: [(values, 0)], 3: [(values, 1)],
                     7: [(mask_back, 0), (mask_back, 1), (mask_back, 2), (mask_back, 3)]}
            for n in range(2 * T + A_LEAD):
                if n == 2 * T + 1:
                    negmax_rows(0)
                score_a(n // (2 * T), n % (2 * T))
                if 3 <= n <= 6:
                    keep_warm(1, 5)
                for step, k in woven.get(n, ()):
                    step(k)
            for p in range(PAIRS):
                for i in range(2 * T):
                    n = (p + 1) * 2 * T + i + A_LEAD
                    if i == 2 * T - 1 and p + 1 < PAIRS:
                        negmax_rows(p + 1)
                    if n < PAIRS * 2 * T:
                        score_a(n // (2 * T), n % (2 * T))
                    score_b(p, i)
                    if (p, i) in ((2, 0), (2, 2)):
                        weighted_values(0, i // 2)
                    if (p, i) == (2, 6):
                        outputs_back(0)
            for half in range(2):
                weighted_values(1, half)
            keep_warm(3, 6)
            for i in range(2):
                pe.wait_ge(S["o_copied"], i + 2)
                for t in (2 * i, 2 * i + 1):
                    last = nc.tensor.transpose(ps[:, i, tok(t)], o_sb[:, tok(t)], ident)
                last.then_inc(S["o_tr"], 1)
            keep_warm(3, 6)
            pe.wait_ge(S["ld_late"], 16)
            for i in range(2):
                pe.wait_ge(S["o_normed"], i + 3)
                for t in (2 * i, 2 * i + 1):
                    last = nc.tensor.transpose(ps[:, 2 + i, (t % 2) * P:(t % 2 + 1) * P], attn[:, t, :], ident)
                last.then_inc(S["at_tr"], 1)
            for i in range(2):
                pe.wait_ge(S["at_copied"], i + 1)
                for t in (2 * i, 2 * i + 1):
                    last = mm(ps[:, 4 + i, (t % 2) * P:(t % 2 + 1) * P], xT[:, tok(t)], l_("wo"))
                last.then_inc(S["op_mm"], 1)
            keep_warm(12, 7)
            for i in range(2):
                for t in (2 * i, 2 * i + 1):
                    pe.wait_ge(S["ln2"], t + 1)
                    last = nc.tensor.transpose(ps[:, i, (t % 2) * P:(t % 2 + 1) * P], xn[:, t, :], ident)
                last.then_inc(S["xT2_tr"], 1)
            def three_terms(out_, a_hi, a_lo, b_hi, b_lo, start, stop):
                mm(out_, a_hi, b_hi, start=start, stop=False)
                mm(out_, a_hi, b_lo, start=False, stop=False)
                return mm(out_, a_lo, b_hi, start=False, stop=stop)

            pe.wait_ge(S["w1_made"], 1)
            pe.wait_ge(S["xT2"], 1)
            for w in (w1_hi, w1_lo):
                for c in range(KT):
                    mm(ps[:, 3 + c, half_cols(0)], w[:, tok(c)], xT_hi[:, half_cols(0)], w is w1_hi, False)
            pe.wait_ge(S["xT2_lo"], 1)
            for c in range(KT):
                mm(ps[:, 3 + c, half_cols(0)], w1_hi[:, tok(c)], xT_lo[:, half_cols(0)], False, True)
            pe.wait_ge(S["xT2_lo"], 2)
            for c in range(KT):
                three_terms(ps[:, 3 + c, half_cols(1)], w1_hi[:, tok(c)], w1_lo[:, tok(c)], xT_hi[:, half_cols(1)],
                            xT_lo[:, half_cols(1)], True, True).then_inc(S["h0_mm"], 1)

            def experts_tile(t, after):
                bank = 2 * ((t + 1) % 2)
                for half in range(2):
                    if t >= 2:
                        pe.wait_ge(S["combined"], 2 * (t - 2) + half + 1)
                    mm(ps[:, bank + half, :], sel[:, 0, :], bd_st[:, half * EH * D:(half + 1) * EH * D], True, False)
                    for k in range(KT):
                        c = 2 * k + half
                        last = three_terms(ps[:, bank + half, :], h_hi[:, k, tok(t)], h_lo[:, k, tok(t)],
                                           w_hi[:, c, :], w_lo[:, c, :], False, k == KT - 1)
                        if k == KT - 1:
                            last.then_inc(S["gm2"], 1)
                        for at, step, tile in after:
                            if at == half * KT + k:
                                step(tile)

            def first_tile():
                pe.wait_ge(S["split"], WD_CHUNKS)
                pe.wait_ge(S["sel_made"], 1)
                pe.wait_ge(S["bd_made"], 1)
                for half in range(2):
                    if half:
                        pe.wait_ge(S["h0_act"], 1)
                    mm(ps[:, 2 + half, :], sel[:, 0, :], bd_st[:, half * EH * D:(half + 1) * EH * D], True, False)

                def low(k):
                    pe.wait_ge(S["h0_lo"], k + 1)
                    for half in range(2):
                        last = mm(ps[:, 2 + half, :], h_lo[:, k, tok(0)], w_hi[:, 2 * k + half, :], False, k == KT - 1)
                        if k == KT - 1:
                            last.then_inc(S["gm2"], 1)

                for k in range(KT):
                    pe.wait_ge(S["h0_hi_a" if k % 2 else "h0_hi"], k // 2 + 1)
                    for half in range(2):
                        for w in (w_hi, w_lo):
                            mm(ps[:, 2 + half, :], h_hi[:, k, tok(0)], w[:, 2 * k + half, :], False, False)
                    if k:
                        low(k - 1)
                low(KT - 1)

            def features_back(t):
                pe.wait_ge(S["xc_made"], t + 1)
                if t == 0:
                    pe.wait_ge(S["lg0_copied"], 1)
                else:
                    pe.wait_ge(S["f_copied"], t)
                nc.tensor.transpose(ps[:, 7, 0:P], xn[:, t, :], ident).then_inc(S["f_tr"], 1)

            def keys_queries(t):
                pe.wait_ge(S["f_copied"], t + 1)
                if t:
                    pe.wait_ge(S["kq_normed"], t)
                    pe.wait_ge(S["q_copied"], t)
                mm(ps[:, 5, 0:2 * D], xT[:, tok(t)], l_("wkq"))
                mm(ps[:, 5, 2 * D:3 * D], l_("wkq")[:, D:2 * D], xT[:, tok(t)]).then_inc(S["kq_mm"], 1)

            def keys_back(t):
                pe.wait_ge(S["kq_normed"], t + 1)
                if t:
                    pe.wait_ge(S["kq_copied"], t)
                nc.tensor.transpose(ps[:, 6, 0:P], kqn[:, t, :], ident).then_inc(S["kq_tr"], 1)

            def logits(_):
                pe.wait_ge(S["wg_made"], 1)
                for k in range(KT):
                    mm(ps[0:2 * E, 7, :], wg_st[:, k, :], h_hi[:, k, :], k == 0, False)
                    last = mm(ps[0:2 * E, 7, :], wg_st[:, k, :], h_lo[:, k, :], False, k == KT - 1)
                last.then_inc(S["lg0_mm"], 1)

            def logits_back(_):
                pe.wait_ge(S["lg0_copied"], 1)
                for t in range(T):
                    last = nc.tensor.transpose(ps[:, 6, t * 2 * E:(t + 1) * 2 * E], lgT[:, tok(t)],
                                               ident[0:2 * E, 0:2 * E])
                last.then_inc(S["lg0_tr"], 1)

            def attention(j, bank, cols):
                mm(ps[:, bank, cols], identb[:, :], maskT[:, j, cols], stop=False)
                mm(ps[:, bank, cols], kqT[:, 1, tok(j)], kqT[:, 0, cols], start=False).then_inc(S["at2_mm"], 1)

            def pv_out(t):
                return ps[:, t // 2, (t % 2) * (D + 2):(t % 2 + 1) * (D + 2)]

            def own_features(t):
                mm(pv_out(t), diag[:, t, :], f_sb[:, t, :], t % 2 == 0, False)

            def propagate(t, j):
                return mm(pv_out(t), prob2[:, j, tok(t)], f_sb[:, j, :], False, t % 2 == 1 and j == T - 1)

            first_tile()
            logits(0)
            experts_tile(1, [(0, logits_back, 0)])
            experts_tile(2, [(4, features_back, 0), (5, keys_queries, 0)])
            experts_tile(3, [(1, features_back, 1), (2, keys_back, 0), (3, keys_queries, 1), (4, features_back, 2),
                             (6, keys_back, 1), (6, keys_queries, 2)])
            last_tile = T - 1
            keep_warm(6, 2)
            keys_back(2)
            pe.wait_ge(S["kq_copied"], last_tile)
            attention(0, 2, old)
            features_back(last_tile)
            attention(1, 3, old)
            keys_queries(last_tile)
            attention(2, 4, old)
            pe.wait_ge(S["combined"], 2 * T)
            pe.wait_ge(S["diag_made"], 1)
            pe.wait_ge(S["fr"], T)
            for t in (0, 1):
                own_features(t)
            for j in range(last_tile):
                pe.wait_ge(S["exp2"], j + 1)
                if j == last_tile - 1:
                    keys_back(last_tile)
                for t in (0, 1):
                    propagate(t, j)
            pe.wait_ge(S["kq_copied"], T)
            attention(last_tile, 7, slice(0, N))
            for j in range(last_tile):
                attention(j, 2 + j, new)
            pe.wait_ge(S["exp2"], T)
            for t in (0, 1):
                last = propagate(t, last_tile)
            last.then_inc(S["pv2"], 1)
            for t in (2, 3):
                own_features(t)
            for j in range(T):
                propagate(2, j)
            propagate(last_tile, last_tile)
            for j in range(last_tile):
                pe.wait_ge(S["exp2"], T + j + 1)
                last = mm(pv_out(last_tile), prob2[:, j, new], f_sb[:, j, :], False, j == last_tile - 1)
            last.then_inc(S["pv2"], 1)
            keep_warm(9, 3)
            for i in range(2):
                for t in (2 * i, 2 * i + 1):
                    pe.wait_ge(S["ln4"], t + 1)
                    last = nc.tensor.transpose(ps[:, 4 + i, (t % 2) * P:(t % 2 + 1) * P], xn[:, t, :], ident)
                last.then_inc(S["xT4_tr"], 1)

            def w1_slot(e):
                return (WD_CHUNKS + 2 * e) % SLOTS

            def w2_slot(e):
                return (WD_CHUNKS + 2 * e + 1) % SLOTS

            def logits1_back():
                pe.wait_ge(S["lg1_copied"], 1)
                for t in range(T):
                    last = nc.tensor.transpose(ps[:, 7, t * 2 * E:(t + 1) * 2 * E], lgT[:, tok(t)],
                                               ident[0:2 * E, 0:2 * E])
                last.then_inc(S["lg1_tr"], 1)

            def hidden(e, between={}):
                pe.wait_ge(S["split"], WD_CHUNKS + 2 * e + 1)
                s = w1_slot(e)
                for i in range(2 if e == 0 else 1):
                    cols = half_cols(i) if e == 0 else slice(0, N)
                    for c in range(KT):
                        if c in between:
                            between[c]()
                        if e:
                            pe.wait_ge(S["h_act"], (e - 1) * KT + c + 1)
                        elif c == 0:
                            pe.wait_ge(S["xT4_lo"], i + 1)
                        last = three_terms(ps[:, (c + 1) % 4, cols], w_hi[:, s, tok(c)], w_lo[:, s, tok(c)],
                                           xT_hi[:, cols], xT_lo[:, cols], True, True)
                        if e or i:
                            last.then_inc(S["h_mm"], 1)

            def expert_out(e, between=None):
                _, high, low = units[e % 2]
                pe.wait_ge(S["split"], WD_CHUNKS + 2 * e + 2)
                s = w2_slot(e)
                for i in range(2 if e == E - 1 else 1):
                    if between and i:
                        between()
                    cols = half_cols(i) if e == E - 1 else slice(0, N)
                    bank = 4 + (e + i) % 2
                    if e >= 2:
                        pe.wait_ge(S["part_made"], e - 1 + i)
                    for c in range(KT):
                        pe.wait_ge(S["h_lo_s"], e * KT + c + 1)
                        last = three_terms(ps[:, bank, cols], w_hi[:, s, tok(c)], w_lo[:, s, tok(c)],
                                           high[:, c, cols], low[:, c, cols], c == 0, c == KT - 1)
                    last.then_inc(S["y_half" if e == E - 1 else "y_mm"], 1)

            def broadcast_weights(e):
                if e == 1:
                    pe.wait_ge(S["gateT_made"], 1)
                if e >= 2:
                    pe.wait_ge(S["wb_made"], e - 1)
                mm(ps[:, 6 + (e + 1) % 2, :], sel[:, e, :], wT_st[:, :]).then_inc(S["wb_mm"], 1)

            def first_broadcast():
                pe.wait_ge(S["w_st"], 1)
                broadcast_weights(0)

            def second_broadcast():
                broadcast_weights(1)

            hidden(0)
            pe.wait_ge(S["wg1_made"], 1)
            mm(ps[0:2 * E, 6, :], wg1_st[:, :], xT_hi[:, :], True, False)
            mm(ps[0:2 * E, 6, :], wg1_st[:, :], xT_lo[:, :], False, True).then_inc(S["lg1_mm"], 1)
            hidden(1, {1: logits1_back})
            expert_out(0)
            hidden(2)
            pe.wait_ge(S["gate1"], 1)
            for t in range(T):
                last = nc.tensor.transpose(ps[0:64, 6, tok(t)], gate[:, t, :], ident)
            last.then_inc(S["w_tr"], 1)
            expert_out(1)
            for e in range(3, E):
                hidden(e, {1: first_broadcast, 3: second_broadcast} if e == 3 else {})
                broadcast_weights(e - 1)
                if e == E - 1:
                    broadcast_weights(e)
                expert_out(e - 1)

            pe.wait_ge(S["ld_bias"], 16)
            pe.wait_ge(S["gateT_made"], 1)
            pe.wait_ge(S["h_act"], E * KT)
            for t in range(T):
                last = mm(ps[:, 0, tok(t)], gateT[:, tok(t)], b2_sb[:, :])
            last.then_inc(S["b2_mm"], 1)

            def turned_sum():
                pe.wait_ge(S["acc_made"], E - 2)
                for t in range(T):
                    last = nc.tensor.transpose(ps[:, 1, tok(t)], acc[:, tok(t)], ident)
                last.then_inc(S["acc_tr"], 1)

            expert_out(E - 1, turned_sum)
            for i in range(2):
                pe.wait_ge(S["part_made"], E + i)
                for t in (2 * i, 2 * i + 1):
                    last = nc.tensor.transpose(ps[:, 2 + i, (t % 2) * P:(t % 2 + 1) * P],
                                               part[:, (E - 1) % 2, tok(t)], ident)
                last.then_inc(S["fin_tr"], 1)


def _layout(inputs):
    import numpy as np

    g = {k: np.asarray(v) for k, v in inputs.items()}
    f = np.float32

    wq0 = np.zeros((D, 4, BLOCK), f)
    bq0 = np.zeros((4, BLOCK), f)
    wq0[:, 0:3] = g["L0_gnn_Wq"].T[:, None, 0:BLOCK]
    bq0[0:3] = g["L0_gnn_bq"][0:BLOCK]
    wk0 = np.zeros((D, 2, 4, BLOCK), f)
    bk0 = np.zeros((2, 4, BLOCK), f)
    for h in range(2):
        a = slice(h * DH, (h + 1) * DH)
        wk0[:, h, 0:3, a] = g["L0_gnn_Wk"].T[:, None, a]
        bk0[h, 0:3, a] = g["L0_gnn_bk"][a]
        bk0[h, 3, h] = 1.0
    wv = np.zeros((D, H, BLOCK), f)
    bv = np.zeros((H, BLOCK), f)
    wv[:, :, 0:DH] = g["L0_gnn_Wv"].T.reshape(D, H, DH)
    bv[:, 0:DH] = g["L0_gnn_bv"].reshape(H, DH)
    bv[:, ONES_COL] = 1.0
    sel = np.zeros((P, E, P), f)
    for e in range(E):
        sel[e, e] = sel[BLOCK + e, e] = 1.0

    early = {
        "ident": np.eye(P, dtype=f),
        "e1": g["L0_gnn_E"][1][:, None],
        "bk0": bk0.reshape(2, P).T,
        "bq0": bq0.reshape(P, 1),
        "wk0": wk0.reshape(D, 2 * P),
        "wq0": wq0.reshape(D, P),
        "bq": g["L0_gnn_bq"][:, None],
        "bk": g["L0_gnn_bk"][:, None],
        "hb1": g["L0_ffn_b1"].reshape(KT, P).T,
        "fb1": g["L1_ffn_b1"].reshape(E * KT, P).T,
        "hnT": g["L0_gnn_h_neigh"].T,
        "wk": g["L0_gnn_Wk"].T,
        "wv": wv.reshape(D, H * BLOCK),
        "wq": g["L0_gnn_Wq"].T,
    }
    late = {
        "wo": g["L0_gnn_Wo"].T,
        "w1": g["L0_ffn_W1"],
        "wg0": g["L0_ffn_Wg"].reshape(KT, P, E).transpose(1, 0, 2).reshape(P, KT * E),
        "wkq": np.concatenate([g["L1_gnn_Wk"].T, g["L1_gnn_Wq"].T], axis=1),
        "wg1": g["L1_ffn_Wg"],
        "sel": sel.reshape(P, E * P),
    }
    rows = {
        "bv": bv.reshape(-1), "bo": g["L0_gnn_bo"], "bg0": g["L0_ffn_bg"], "bg1": g["L1_ffn_bg"],
        "iota": np.arange(E, dtype=f),
    }
    wd = g["L0_ffn_Wd"].reshape(2, EH, KT, P, D).transpose(2, 0, 3, 1, 4).reshape(WD_CHUNKS, P, EH * D)
    w2 = g["L1_ffn_W2"].reshape(E, KT, P, D).transpose(0, 2, 1, 3).reshape(E, P, KT * D)
    w12 = np.stack([g["L1_ffn_W1"], w2], axis=1).reshape(2 * E, P, HID)
    return {
        "x": g["x"],
        "adj": g["adj"],
        "early": np.concatenate([early[k] for k in EARLY], axis=1),
        "late": np.concatenate([late[k] for k in LATE], axis=1),
        "rows": np.concatenate([rows[k] for k in ROWS]),
        "bd": g["L0_ffn_bd"].reshape(-1),
        "b2": g["L1_ffn_b2"],
        "chunks": np.concatenate([wd, w12], axis=0),
    }


def kernel(**inputs):
    import numpy as np
    import concourse.bacc as bacc
    from concourse.bass_utils import run_bass_kernel_spmd

    nc = bacc.Bacc("TRN2", target_bir_lowering=False, num_devices=1)
    arrays, args = {}, []
    for name, a in _layout(inputs).items():
        a = np.ascontiguousarray(a)
        arrays[f"in_{name}"] = a
        args.append(nc.dram_tensor(f"in_{name}", a.shape, mybir.dt.from_np(a.dtype), kind="ExternalInput").ap())
    args.append(nc.dram_tensor("out_x", (N, D), F32, kind="ExternalOutput").ap())
    build(nc, *args)
    r = run_bass_kernel_spmd(nc, [arrays], core_ids=[0])
    return r.results[0]["out_x"]
```
